# Optimizing a Trainium2 kernel written in Bass

```python
import numpy as np
import jax
import jax.numpy as jnp

def _softmax(x, axis=-1):
    return jax.nn.softmax(x, axis=axis)

def _gelu(x):
    return jax.nn.gelu(x, approximate=True)

def _silu(x):
    return jax.nn.silu(x)

def _sigmoid(x):
    return jax.nn.sigmoid(x)

def _layernorm(x, axis=-1, eps=1e-05):
    m = jnp.mean(x, axis=axis, keepdims=True)
    v = jnp.var(x, axis=axis, keepdims=True)
    return (x - m) / jnp.sqrt(v + eps)

def _scatter_add(tgt, idx, src, axis=0):
    return tgt.at[idx].add(src)

def _segment_sum(src, seg, n):
    return jax.ops.segment_sum(src, seg, n)
kernel_name = 'mk_macaron_d1_jaxref_r4_499d14'

def setup_inputs(seed: int=0):
    np.random.seed(seed)
    _w = jnp.asarray

    def _L0_attn_setup():
        import jax, jax.numpy as jnp
        import numpy as np
        from jax import lax
        D_MODEL = 256
        D_STATE = 64
        D_CONV = 4
        EXPAND = 2
        D_INNER = D_MODEL * EXPAND
        BATCH = 2
        T = 256
        EPS = 1e-05
        key = jax.random.key(seed)
        ks = jax.random.split(key, 8)
        s = 0.02
        return {'x': jax.random.normal(ks[0], (BATCH, T, D_MODEL), jnp.float32), 'norm_w': jnp.ones((D_MODEL,), jnp.float32), 'norm_b': jnp.zeros((D_MODEL,), jnp.float32), 'Win': jax.random.normal(ks[1], (D_MODEL, 2 * D_INNER), jnp.float32) * s, 'conv_w': jax.random.normal(ks[2], (D_INNER, 1, D_CONV), jnp.float32) * s, 'conv_b': jnp.zeros((D_INNER,), jnp.float32), 'dt_w': jax.random.normal(ks[3], (D_INNER, D_INNER), jnp.float32) * s, 'dt_b': jnp.zeros((D_INNER,), jnp.float32), 'A_log': jnp.broadcast_to(jnp.log(jnp.arange(1, D_STATE + 1, dtype=jnp.float32))[None, :], (D_INNER, D_STATE)).copy(), 'D': jnp.ones((D_INNER,), jnp.float32), 'Bp': jax.random.normal(ks[4], (D_INNER, D_STATE), jnp.float32) * s, 'Cp': jax.random.normal(ks[5], (D_INNER, D_STATE), jnp.float32) * s, 'Wout': jax.random.normal(ks[6], (D_INNER, D_MODEL), jnp.float32) * s}
    _L0_attn_in = _L0_attn_setup()

    def _L0_ffn_setup():
        import jax, jax.numpy as jnp
        import numpy as np
        INT4_QMAX = 7.0

        def simulate_quantize_int4(w):
            scale = jnp.max(jnp.abs(w)) / INT4_QMAX
            q = jnp.clip(jnp.round(w / scale), -8.0, 7.0)
            return q * scale
        key = jax.random.key(seed)
        k_x, k_w, k_bias, k_a, k_b = jax.random.split(key, 5)
        d_in, features, rank = (256, 256, 16)
        x = jax.random.normal(k_x, (4, 2048, d_in), dtype=jnp.float32)
        kernel = jax.random.normal(k_w, (d_in, features), dtype=jnp.float32)
        bias = jax.random.normal(k_bias, (features,), dtype=jnp.float32)
        a = jax.random.normal(k_a, (d_in, rank), dtype=jnp.float32) * (1.0 / np.sqrt(d_in))
        b = jax.random.normal(k_b, (rank, features), dtype=jnp.float32) * 0.01
        return {'x': x, 'kernel': kernel, 'bias': bias, 'a': a, 'b': b}
    _L0_ffn_in = _L0_ffn_setup()
    _d = {'L0_attn_x': _L0_attn_in['x'], 'L0_attn_norm_w': _L0_attn_in['norm_w'], 'L0_attn_norm_b': _L0_attn_in['norm_b'], 'L0_attn_Win': _L0_attn_in['Win'], 'L0_attn_conv_w': _L0_attn_in['conv_w'], 'L0_attn_conv_b': _L0_attn_in['conv_b'], 'L0_attn_dt_w': _L0_attn_in['dt_w'], 'L0_attn_dt_b': _L0_attn_in['dt_b'], 'L0_attn_A_log': _L0_attn_in['A_log'], 'L0_attn_D': _L0_attn_in['D'], 'L0_attn_Bp': _L0_attn_in['Bp'], 'L0_attn_Cp': _L0_attn_in['Cp'], 'L0_attn_Wout': _L0_attn_in['Wout'], 'L0_ffn_kernel': _L0_ffn_in['kernel'], 'L0_ffn_bias': _L0_ffn_in['bias'], 'L0_ffn_a': _L0_ffn_in['a'], 'L0_ffn_b': _L0_ffn_in['b']}
    _x0 = _d['L0_attn_x']
    _d['L0_attn_x'] = jax.random.normal(jax.random.fold_in(jax.random.key(seed), 1), (16, 512, 256), dtype=_x0.dtype)
    del _x0
    return _d

def reference(L0_attn_x, L0_attn_norm_w, L0_attn_norm_b, L0_attn_Win, L0_attn_conv_w, L0_attn_conv_b, L0_attn_dt_w, L0_attn_dt_b, L0_attn_A_log, L0_attn_D, L0_attn_Bp, L0_attn_Cp, L0_attn_Wout, L0_ffn_kernel, L0_ffn_bias, L0_ffn_a, L0_ffn_b):

    def _L0_attn_ref(x, norm_w, norm_b, Win, conv_w, conv_b, dt_w, dt_b, A_log, D, Bp, Cp, Wout):
        import jax, jax.numpy as jnp
        import numpy as np
        from jax import lax
        D_MODEL = 256
        D_STATE = 64
        D_CONV = 4
        EXPAND = 2
        D_INNER = D_MODEL * EXPAND
        BATCH = 2
        T = 256
        EPS = 1e-05
        B_sz, T_len, _ = x.shape
        mu = jnp.mean(x, -1, keepdims=True)
        var = jnp.mean(jnp.square(x - mu), -1, keepdims=True)
        h = (x - mu) * lax.rsqrt(var + EPS) * norm_w + norm_b
        xz = h @ Win
        x_ssm, z = jnp.split(xz, 2, axis=-1)
        xc = jnp.pad(x_ssm, ((0, 0), (D_CONV - 1, 0), (0, 0))).transpose(0, 2, 1)
        xconv = lax.conv_general_dilated(xc, conv_w, (1,), 'VALID', dimension_numbers=('NCH', 'OIH', 'NCH'), feature_group_count=D_INNER)
        x_ssm = jax.nn.silu(xconv.transpose(0, 2, 1) + conv_b)
        dt = jax.nn.softplus(x_ssm @ dt_w + dt_b)
        A = -jnp.exp(A_log)
        Bt = x_ssm @ Bp
        Ct = x_ssm @ Cp

        def step(state, inp):
            x_t, dt_t, B_t, C_t = inp
            dA = jnp.exp(dt_t[:, :, None] * A[None])
            state = state * dA + (dt_t * x_t)[:, :, None] * B_t[:, None, :]
            y_t = jnp.einsum('bds,bs->bd', state, C_t)
            return (state, y_t)
        state0 = jnp.zeros((B_sz, D_INNER, D_STATE), x.dtype)
        xs = (x_ssm.transpose(1, 0, 2), dt.transpose(1, 0, 2), Bt.transpose(1, 0, 2), Ct.transpose(1, 0, 2))
        _, ys = lax.scan(step, state0, xs)
        y = ys.transpose(1, 0, 2)
        y = y + x_ssm * D[None, None, :]
        y = y * jax.nn.silu(z)
        return x + y @ Wout

    def _L0_ffn_ref(x, kernel, bias, a, b):
        import jax, jax.numpy as jnp
        import numpy as np
        INT4_QMAX = 7.0

        def simulate_quantize_int4(w):
            scale = jnp.max(jnp.abs(w)) / INT4_QMAX
            q = jnp.clip(jnp.round(w / scale), -8.0, 7.0)
            return q * scale
        w = simulate_quantize_int4(kernel)
        y = jnp.einsum('bsd,df->bsf', x, w) + bias
        lora = jnp.einsum('bsr,rf->bsf', jnp.einsum('bsd,dr->bsr', x, a), b)
        return y + lora
    x = L0_attn_x
    x = x + 0.5 * _L0_ffn_ref(_layernorm(x, axis=-1), L0_ffn_kernel, L0_ffn_bias, L0_ffn_a, L0_ffn_b)
    x = x + _L0_attn_ref(_layernorm(x, axis=-1), L0_attn_norm_w, L0_attn_norm_b, L0_attn_Win, L0_attn_conv_w, L0_attn_conv_b, L0_attn_dt_w, L0_attn_dt_b, L0_attn_A_log, L0_attn_D, L0_attn_Bp, L0_attn_Cp, L0_attn_Wout)
    x = x + 0.5 * _L0_ffn_ref(_layernorm(x, axis=-1), L0_ffn_kernel, L0_ffn_bias, L0_ffn_a, L0_ffn_b)
    return x

_drawn_inputs = setup_inputs


def setup_inputs(seed=0):
    import zlib

    import numpy as np

    out = dict(_drawn_inputs(seed))
    spreads = {'L0_attn_norm_w': (1.0, 0.6),
     'L0_attn_norm_b': (0.0, 0.8),
     'L0_attn_conv_b': (0.0, 0.8),
     'L0_attn_dt_b': (0.0, 0.8),
     'L0_attn_D': (1.0, 0.6)}
    factors = {'L0_attn_Win': 8.0,
     'L0_attn_conv_w': 8.0,
     'L0_attn_dt_w': 8.0,
     'L0_attn_A_log': 8.0,
     'L0_attn_Bp': 8.0,
     'L0_attn_Cp': 8.0,
     'L0_attn_Wout': 8.0,
     'L0_ffn_a': 8.0,
     'L0_ffn_b': 8.0}
    for name, (base, spread) in spreads.items():
        noise = np.random.default_rng([zlib.crc32(name.encode()), seed]).standard_normal(out[name].shape)
        drawn = base * np.exp(spread * noise) if base else spread * noise
        out[name] = jnp.asarray(drawn.astype(out[name].dtype))
    for name, factor in factors.items():
        out[name] = (out[name] * factor).astype(out[name].dtype)
    return out
```

```python
from contextlib import ExitStack

import concourse.bass as bass
from concourse import mybir

P = 128
NB, T, DM = 16, 512, 256
DI, DS, DC = 512, 64, 4
RANK = 16
EPS = 1e-5
QMAX = 7.0
ROUND = 12582912.0
KM, KI, NJ = DM // P, DI // P, T // P
GS = 4
SB = 8
NBLK = DS // SB
GPB = SB // GS
GB = KI * GPB
GN = NBLK * GB
START = 16
DAR, HR = 2, 4

fp32 = mybir.dt.float32
ALU = mybir.AluOpType
ACT = mybir.ActivationFunctionType
AX = mybir.AxisListType


def at(n):
    return START + n


def begin(nc, counters):
    with nc.Block() as block:
        @block.sync
        def _(sp):
            for s in counters:
                sp.sem_inc(s, START)


def tools(nc, ctx, counters=None):
    def sb(name, shape, dt=fp32):
        return ctx.enter_context(nc.sbuf_tensor(name, shape, dt))

    def pb(name, shape, dt=fp32):
        return ctx.enter_context(nc.psum_tensor(name, shape, dt))

    def sem(name):
        s = ctx.enter_context(nc.semaphore(name))
        if counters is not None:
            counters.append(s)
        return s

    return sb, pb, sem


def constants(nc, sb, pb, sem, w, c):
    wk, aT, lb = sb("wk", [P, KM, DM]), sb("aT", [RANK, DM]), sb("lb", [RANK, DM])
    wabs, wq = sb("wabs", [P, KM, DM]), sb("wq", [P, KM, DM])
    mx, mx1, one, sc, alog = sb("mx", [P, 1]), sb("mx1", [1, 1]), sb("one", [1, P]), sb("sc", [P, 4]), sb("alog", [P, KI, DS])
    biasr = sb("biasr", [1, DM])
    pm, pab = pb("pm", [P, 512]), pb("pab", [P, KM, DM])
    k_small, k_big, k_id, k_abs, k_chain = sem("k_small"), sem("k_big"), sem("k_id"), sem("k_abs"), sem("k_chain")
    k_row, k_col, k_ab, k_one, k_expA, k_d = sem("k_row"), sem("k_col"), sem("k_ab"), sem("k_one"), sem("k_expA"), sem("k_d")

    with nc.Block() as block:
        @block.sync
        def _(sp):
            small = [(wk[:, :, :], w["kernel"].rearrange("(k p) f -> p k f", p=P)), (aT[:, :], w["aT"]), (lb[:, :], w["b"]),
                     (biasr[:, :], w["bias"].rearrange("(o f) -> o f", o=1)),
                     (alog[:, :, :], w["A_log"].rearrange("(k p) s -> p k s", p=P)),
                     (c["conv_w"][:, :, :], w["conv_w"].rearrange("(k p) o j -> p k (o j)", p=P))]
            small += [(c[n][:, :], w[n].rearrange("(k p) -> p k", p=P)) for n in ("conv_b", "dt_b", "D", "norm_w", "norm_b")]
            with nc.allow_non_contiguous_dma(reason="a few KiB, once"):
                for dst, src in small:
                    sp.dma_start(dst, src).then_inc(k_small, 16)
            for dst, src in ((c["Win"][:, :, :], w["Win"].rearrange("(k p) m -> p k m", p=P)),
                             (c["dt_w"][:, :, :], w["dt_w"].rearrange("(k p) m -> p k m", p=P)),
                             (c["bc_w"][:, :, 0:DS], w["Bp"].rearrange("(k p) m -> p k m", p=P)),
                             (c["bc_w"][:, :, DS:2 * DS], w["Cp"].rearrange("(k p) m -> p k m", p=P)),
                             (c["Wout"][:, :, :], w["Wout"].rearrange("(k p) m -> p k m", p=P))):
                sp.dma_start(dst, src).then_inc(k_big, 16)
            sp.wait_ge(k_big, 5 * 16)
            sp.wait_ge(k_small, 11 * 16)

        @block.gpsimd
        def _(pool):
            nc.gpsimd.memset(c["ident"][:, :], 0.0).then_inc(k_id, 1)
            pool.wait_ge(k_id, 1)
            nc.gpsimd.affine_select(out=c["ident"][:, :], in_=c["ident"][:, :], compare_op=ALU.not_equal, fill=1.0,
                                    base=0, pattern=[[-1, P]], channel_multiplier=1).then_inc(k_id, 1)

        @block.scalar
        def _(act):
            act.wait_ge(k_small, 11 * 16)
            nc.scalar.activation(wabs[:, :, :], wk[:, :, :], ACT.Abs).then_inc(k_abs, 1)
            nc.scalar.activation(c["negA"][:, :, :], alog[:, :, :], ACT.Exp).then_inc(k_expA, 1)

        @block.tensor
        def _(pe):
            pe.wait_ge(k_id, 2)
            pe.wait_ge(k_chain, 1)
            nc.tensor.matmul(pm[0:1, 0:P], mx[:, :], c["ident"][:, :], start=True, stop=True).then_inc(k_row, 1)
            pe.wait_ge(k_one, 1)
            pe.wait_ge(k_chain, 2)
            nc.tensor.matmul(pm[:, P:P + 1], one[:, :], mx1[:, :], start=True, stop=True).then_inc(k_col, 1)
            pe.wait_ge(k_small, 11 * 16)
            for k in range(KM):
                nc.tensor.matmul(pab[:, k, :], aT[:, k * P:(k + 1) * P], lb[:, :], start=(k == 0), stop=(k == KM - 1),
                                 skip_group_check=True).then_inc(k_ab, 1)

        @block.vector
        def _(dve):
            n = [0]

            def link(ins):
                n[0] += 1
                ins.then_inc(k_chain, 1)
                dve.wait_ge(k_chain, n[0])

            nc.vector.memset(one[:, :], 1.0).then_inc(k_one, 1)
            dve.wait_ge(k_abs, 1)
            link(nc.vector.reduce_max(mx[:, :], wabs[:, :, :].rearrange("p k f -> p (k f)"), AX.X))
            dve.wait_ge(k_row, 1)
            link(nc.vector.reduce_max(mx1[:, :], pm[0:1, 0:P], AX.X))
            dve.wait_ge(k_col, 1)
            link(nc.vector.tensor_scalar(sc[:, 0:1], pm[:, P:P + 1], 1.0 / QMAX, None, ALU.mult))
            link(nc.vector.reciprocal(sc[:, 1:2], sc[:, 0:1]))
            link(nc.vector.tensor_scalar(sc[:, 2:3], sc[:, 0:1], 0.5, None, ALU.mult))
            link(nc.vector.tensor_scalar(wq[:, :, :], wk[:, :, :], sc[:, 1:2], ROUND, ALU.mult, ALU.add))
            link(nc.vector.tensor_scalar(wabs[:, :, :], wq[:, :, :], ROUND, QMAX, ALU.subtract, ALU.min))
            link(nc.vector.tensor_scalar(wq[:, :, :], wabs[:, :, :], -8.0, sc[:, 2:3], ALU.max, ALU.mult))
            dve.wait_ge(k_ab, KM)
            link(nc.vector.scalar_tensor_tensor(out=c["Wf"][:, :, :], in0=pab[:, :, :], scalar=0.5, in1=wq[:, :, :],
                                                op0=ALU.mult, op1=ALU.add))
            dve.wait_ge(k_small, 11 * 16)
            link(nc.vector.tensor_scalar(c["bias"][:, :], biasr[:, :], 0.5, None, ALU.mult))
            link(nc.vector.tensor_copy(c["ones"][:, :], one[:, :]))
            dve.wait_ge(k_expA, 1)
            link(nc.vector.tensor_scalar(c["negA"][:, :, :], c["negA"][:, :, :], -1.0, None, ALU.mult))
            dve.wait_ge(k_id, 2)
            for k in range(KI):
                nc.vector.tensor_scalar(c["diagD"][:, k, :], c["ident"][:, :], c["D"][:, k:k + 1], None, ALU.mult).then_inc(k_d, 1)


def deviation(nc, act, tag, root, mv, sd, count):
    act.wait_ge(tag, at(count + 2))
    nc.scalar.activation(sd[:, :], mv[:, :, 1], ACT.Sqrt, bias=EPS).then_inc(root, 1)


def layer_norm(nc, dve, tag, root, xs, out, st, mv, sd, rs, n, count, seq):
    for j in range(NJ):
        last = nc.vector.bn_stats(st[:, j, :], xs[:, j, :])
    last.then_inc(tag, 1)
    dve.wait_ge(tag, at(count + 1))
    nc.vector.memset(rs[:, :], 0.0)
    for j in range(NJ):
        last = nc.vector.bn_aggr(mv[:, j, :], st[:, j, :])
    last.then_inc(tag, 1)
    dve.wait_ge(tag, at(count + 2))
    dve.wait_ge(root, at(seq + 1))
    nc.vector.reciprocal(rs[:, :], sd[:, :]).then_inc(tag, 1)
    dve.wait_ge(tag, at(count + 3))
    for j in range(NJ):
        nc.vector.tensor_scalar(out[:, j, :], xs[:, j, :], mv[:, j, 0:1], rs[:, j:j + 1], ALU.subtract,
                                ALU.mult).then_inc(n, 1)


def first_ffn(nc, sb, pb, sem, counters, w, c, dram):
    X, xn, x1 = sb("a_x", [P, NJ, DM]), sb("a_xn", [P, NJ, DM]), sb("a_x1", [P, NJ, DM])
    xa, xh, R = sb("a_xa", [P, NJ, DM]), sb("a_xh", [P, NJ, DM]), sb("a_r", [P, NJ, DM])
    xnT, hT = sb("a_xnT", [P, KM, T]), sb("a_hT", [P, KM, T])
    st, mv, rs = sb("a_st", [P, NJ, 6]), sb("a_mv", [P, NJ, 2]), sb("a_rs", [P, NJ])
    sd = sb("a_sd", [P, NJ])
    pT = [pb(f"a_pT{i}", [P, KM, 256]) for i in range(2)]
    pF = [pb(f"a_pF{i}", [P, 512]) for i in range(2)]
    pH = [pb(f"a_pH{i}", [P, KM, 256]) for i in range(2)]
    x_in, ln1, ln2, ln3 = sem("a_x_in"), sem("a_ln1"), sem("a_ln2"), sem("a_ln3")
    n1, n2, n3, x1_done, r_done = sem("a_n1"), sem("a_n2"), sem("a_n3"), sem("a_x1_done"), sem("a_r_done")
    t1, t1_out, ffn, t2, h_out = sem("a_t1"), sem("a_t1_out"), sem("a_ffn"), sem("a_t2"), sem("a_h_out")
    h_st, r_st = sem("a_h_st"), sem("a_r_st")
    rt1, rt2, rt3 = sem("a_rt1"), sem("a_rt2"), sem("a_rt3")

    begin(nc, counters)
    with nc.Block() as block:
        @block.sync
        def _(sp):
            with sp.Fori(0, NB) as b:
                sp.wait_ge(x1_done, at(NJ * b))
                sp.dma_start(X[:, :, :], dram["x"][bass.ds(b, 1)].rearrange("o (j p) d -> p (o j) d", p=P)).then_inc(x_in, 16)
                sp.wait_ge(r_done, at(b + 1))
                sp.dma_start(dram["r"][bass.ds(b, 1)].rearrange("o (j p) d -> p (o j) d", p=P), R[:, :, :]).then_inc(r_st, 16)
                sp.wait_ge(h_out, at(NJ * KM * b + NJ * KM))
                sp.dma_start(dram["hT"][bass.ds(b, 1)].rearrange("o k p t -> p (o k) t"), hT[:, :, :]).then_inc(h_st, 16)
            sp.wait_ge(r_st, at(16 * NB))
            sp.wait_ge(h_st, at(16 * NB))

        @block.vector
        def _(dve):
            with dve.Fori(0, NB) as b:
                dve.wait_ge(x_in, at(16 * b + 16))
                dve.wait_ge(t1, at(NJ * b))
                layer_norm(nc, dve, ln1, rt1, X, xn, st, mv, sd, rs, n1, 3 * b, b)
                dve.wait_ge(r_done, at(b))
                for j in range(NJ):
                    dve.wait_ge(ffn, at(NJ * b + j + 1))
                    nc.vector.tensor_tensor(x1[:, j, :], X[:, j, :], pF[j % 2][:, 0:DM], ALU.add).then_inc(x1_done, 1)
                dve.wait_ge(x1_done, at(NJ * b + NJ))
                dve.wait_ge(n1, at(NJ * b + NJ))
                layer_norm(nc, dve, ln2, rt2, x1, xa, st, mv, sd, rs, n2, 3 * b, b)
                dve.wait_ge(n2, at(NJ * b + NJ))
                dve.wait_ge(t2, at(NJ * b))
                layer_norm(nc, dve, ln3, rt3, xa, xh, st, mv, sd, rs, n3, 3 * b, b)
                dve.wait_ge(n3, at(NJ * b + NJ))

        @block.gpsimd
        def _(pool):
            with pool.Fori(0, NB) as b:
                pool.wait_ge(n2, at(NJ * b + NJ))
                pool.wait_ge(r_st, at(16 * b))
                nc.gpsimd.tensor_tensor(R[:, :, :], x1[:, :, :], xa[:, :, :], ALU.add).then_inc(r_done, 1)

        @block.tensor
        def _(pe):
            with pe.Fori(0, NB) as b:
                def ffn_mm(j):
                    pe.wait_ge(t1_out, at(KM * (NJ * b + j + 1)))
                    if j < 2:
                        pe.wait_ge(x1_done, at(NJ * b))
                    else:
                        pe.wait_ge(x1_done, at(NJ * b + j - 1))
                    nc.tensor.matmul(pF[j % 2][:, 0:DM], c["ones"][:, :], c["bias"][:, :], start=True, stop=False)
                    for k in range(KM):
                        last = nc.tensor.matmul(pF[j % 2][:, 0:DM], xnT[:, k, j * P:(j + 1) * P], c["Wf"][:, k, :],
                                                start=False, stop=(k == KM - 1))
                    last.then_inc(ffn, 1)

                for j in range(NJ):
                    pe.wait_ge(n1, at(NJ * b + j + 1))
                    if j < 2:
                        pe.wait_ge(t1_out, at(KM * NJ * b))
                    else:
                        pe.wait_ge(t1_out, at(KM * (NJ * b + j - 1)))
                    for k in range(KM):
                        last = nc.tensor.transpose(pT[j % 2][:, k, 0:P], xn[:, j, k * P:(k + 1) * P], c["ident"][:, :])
                    last.then_inc(t1, 1)
                    if j:
                        ffn_mm(j - 1)
                ffn_mm(NJ - 1)
                for j in range(NJ):
                    pe.wait_ge(n3, at(NJ * b + j + 1))
                    if j < 2:
                        pe.wait_ge(h_out, at(KM * NJ * b))
                    else:
                        pe.wait_ge(h_out, at(KM * (NJ * b + j - 1)))
                    for k in range(KM):
                        last = nc.tensor.transpose(pH[j % 2][:, k, 0:P], xh[:, j, k * P:(k + 1) * P], c["ident"][:, :])
                    last.then_inc(t2, 1)

        @block.scalar
        def _(act):
            with act.Fori(0, NB) as b:
                deviation(nc, act, ln1, rt1, mv, sd, 3 * b)
                act.wait_ge(ffn, at(NJ * b))
                for j in range(NJ):
                    act.wait_ge(t1, at(NJ * b + j + 1))
                    for k in range(KM):
                        nc.scalar.activation(xnT[:, k, j * P:(j + 1) * P], pT[j % 2][:, k, 0:P], ACT.Copy).then_inc(t1_out, 1)
                deviation(nc, act, ln2, rt2, mv, sd, 3 * b)
                deviation(nc, act, ln3, rt3, mv, sd, 3 * b)
                act.wait_ge(h_st, at(16 * b))
                for j in range(NJ):
                    act.wait_ge(t2, at(NJ * b + j + 1))
                    for k in range(KM):
                        nc.scalar.activation(hT[:, k, j * P:(j + 1) * P], pH[j % 2][:, k, 0:P], ACT.Identity,
                                             scale=c["norm_w"][:, k:k + 1], bias=c["norm_b"][:, k:k + 1]).then_inc(h_out, 1)


def projections(nc, sb, pb, sem, counters, w, c, dram):
    hT = sb("p_hT", [P, KM, T])
    xs = sb("p_xs", [P, KI, DC - 1 + T])
    cv, U, Z = sb("p_cv", [P, KI, T]), sb("p_u", [P, KI, T]), sb("p_z", [P, KI, T])
    ab, ee, ln, w1, re = (sb(f"p_{n}", [P, KI, T]) for n in ("ab", "ee", "ln", "w1", "re"))
    uu = sb("p_uu", [P, KI, T])
    BC = sb("p_bc", [P, T])
    pX = [pb(f"p_pX{m}", [P, T]) for m in range(KI)]
    pZ = [pb(f"p_pZ{m}", [P, T]) for m in range(KI)]
    names = ("h_in", "zero", "mm_x", "mm_z", "mm_dt", "mm_bc", "xs_out", "conv", "u_done", "z_done", "abs_done", "relu_done", "exp_done",
             "ln_done", "w1_done", "soft1", "soft2", "dt_done", "uu_done", "bc_out", "u_st", "z_st", "dt_st", "uu_st", "bc_st")
    s = {n: sem("p_" + n) for n in names}

    def tile_of(d, b, m):
        return dram[d][bass.ds(b, 1), m * P:(m + 1) * P, :].rearrange("o p t -> p (o t)")

    begin(nc, counters)
    with nc.Block() as block:
        @block.sync
        def _(sp):
            sp.dma_start(hT[:, :, :], dram["hT"][0:1].rearrange("o k p t -> p (o k) t")).then_inc(s["h_in"], 16)

            def sequence(b, more):
                for m in range(KI):
                    sp.wait_ge(s["u_done"], at(KI * b + m + 1))
                    sp.dma_start(tile_of("u", b, m), U[:, m, :]).then_inc(s["u_st"], 16)
                for m in range(KI):
                    sp.wait_ge(s["z_done"], at(KI * b + m + 1))
                    sp.dma_start(tile_of("z", b, m), Z[:, m, :]).then_inc(s["z_st"], 16)
                if more:
                    sp.wait_ge(s["mm_z"], at(KI * b + KI))
                    sp.dma_start(hT[:, :, :], dram["hT"][bass.ds(b + 1, 1)].rearrange("o k p t -> p (o k) t")).then_inc(s["h_in"], 16)
                sp.wait_ge(s["bc_out"], at(b + 1))
                sp.dma_start(dram["bc"][bass.ds(b, 1)].rearrange("o p t -> p (o t)"), BC[:, :]).then_inc(s["bc_st"], 16)
                for m in range(KI):
                    sp.wait_ge(s["dt_done"], at(KI * b + m + 1))
                    sp.dma_start(tile_of("dt", b, m), ab[:, m, :]).then_inc(s["dt_st"], 16)
                    sp.wait_ge(s["uu_done"], at(KI * b + m + 1))
                    sp.dma_start(tile_of("uu", b, m), uu[:, m, :]).then_inc(s["uu_st"], 16)

            with sp.Fori(0, NB - 1) as b:
                sequence(b, True)
            sequence(NB - 1, False)
            for n in ("u_st", "z_st", "dt_st", "uu_st"):
                sp.wait_ge(s[n], at(16 * KI * NB))
            sp.wait_ge(s["bc_st"], at(16 * NB))

        @block.tensor
        def _(pe):
            with pe.Fori(0, NB) as b:
                pe.wait_ge(s["h_in"], at(16 * b + 16))
                for m in range(KI):
                    pe.wait_ge(s["abs_done"], at(KI * b))
                    pe.wait_ge(s["relu_done"], at(KI * b))
                    for k in range(KM):
                        last = nc.tensor.matmul(pX[m][:, :], c["Win"][:, k, m * P:(m + 1) * P], hT[:, k, :],
                                                start=(k == 0), stop=(k == KM - 1))
                    last.then_inc(s["mm_x"], 1)
                for m in range(KI):
                    pe.wait_ge(s["z_done"], at(KI * b))
                    pe.wait_ge(s["bc_out"], at(b))
                    for k in range(KM):
                        last = nc.tensor.matmul(pZ[m][:, :], c["Win"][:, k, DI + m * P:DI + (m + 1) * P], hT[:, k, :],
                                                start=(k == 0), stop=(k == KM - 1))
                    last.then_inc(s["mm_z"], 1)
                pe.wait_ge(s["u_done"], at(KI * b + KI))
                pe.wait_ge(s["z_done"], at(KI * b + 1))
                for k in range(KI):
                    last = nc.tensor.matmul(pZ[0][:, :], c["bc_w"][:, k, :], U[:, k, :], start=(k == 0), stop=(k == KI - 1))
                last.then_inc(s["mm_bc"], 1)
                for m in range(KI):
                    pe.wait_ge(s["xs_out"], at(KI * b + m + 1))
                    for k in range(KI):
                        last = nc.tensor.matmul(pX[m][:, :], c["dt_w"][:, k, m * P:(m + 1) * P], U[:, k, :],
                                                start=(k == 0), stop=(k == KI - 1))
                    last.then_inc(s["mm_dt"], 1)

        @block.scalar
        def _(act):
            act.wait_ge(s["zero"], at(1))
            with act.Fori(0, NB) as b:
                def take_xs(m):
                    act.wait_ge(s["mm_x"], at(KI * b + m + 1))
                    act.wait_ge(s["conv"], at(DC * KI * b))
                    nc.scalar.activation(xs[:, m, DC - 1:], pX[m][:, :], ACT.Copy).then_inc(s["xs_out"], 1)

                def silu_u(m):
                    act.wait_ge(s["conv"], at(DC * (KI * b + m + 1)))
                    act.wait_ge(s["mm_dt"], at(KI * b))
                    act.wait_ge(s["uu_done"], at(KI * b))
                    act.wait_ge(s["u_st"], at(16 * KI * b))
                    nc.scalar.activation(U[:, m, :], cv[:, m, :], ACT.Silu).then_inc(s["u_done"], 1)

                def silu_z(m):
                    act.wait_ge(s["mm_z"], at(KI * b + m + 1))
                    act.wait_ge(s["z_st"], at(16 * KI * b))
                    nc.scalar.activation(Z[:, m, :], pZ[m][:, :], ACT.Silu).then_inc(s["z_done"], 1)

                take_xs(0)
                take_xs(1)
                take_xs(2)
                silu_u(0)
                take_xs(3)
                silu_u(1)
                silu_z(0)
                silu_u(2)
                silu_z(1)
                silu_u(3)
                silu_z(2)
                silu_z(3)
                act.wait_ge(s["mm_bc"], at(b + 1))
                act.wait_ge(s["bc_st"], at(16 * b))
                nc.scalar.activation(BC[:, :], pZ[0][:, :], ACT.Copy).then_inc(s["bc_out"], 1)
                for m in range(KI):
                    act.wait_ge(s["mm_dt"], at(KI * b + m + 1))
                    act.wait_ge(s["dt_st"], at(16 * KI * b))
                    act.wait_ge(s["uu_done"], at(KI * b))
                    nc.scalar.activation(ab[:, m, :], pX[m][:, :], ACT.Abs, bias=c["dt_b"][:, m:m + 1]).then_inc(s["abs_done"], 1)
                    act.wait_ge(s["dt_done"], at(KI * b))
                    nc.scalar.activation(re[:, m, :], pX[m][:, :], ACT.Relu, bias=c["dt_b"][:, m:m + 1]).then_inc(s["relu_done"], 1)
                    act.wait_ge(s["abs_done"], at(KI * b + m + 1))
                    nc.scalar.activation(ee[:, m, :], ab[:, m, :], ACT.Exp, scale=-1.0).then_inc(s["exp_done"], 1)
                    act.wait_ge(s["exp_done"], at(KI * b + m + 1))
                    nc.scalar.activation(ln[:, m, :], ee[:, m, :], ACT.Ln, bias=1.0).then_inc(s["ln_done"], 1)
                    nc.scalar.activation(w1[:, m, :], ee[:, m, :], ACT.Copy, bias=1.0).then_inc(s["w1_done"], 1)

        @block.vector
        def _(dve):
            nc.vector.memset(xs[:, :, 0:DC - 1], 0.0).then_inc(s["zero"], 1)
            dve.wait_ge(s["zero"], at(1))
            with dve.Fori(0, NB) as b:
                for m in range(KI):
                    n = DC * (KI * b + m)
                    dve.wait_ge(s["xs_out"], at(KI * b + m + 1))
                    dve.wait_ge(s["u_done"], at(KI * b + m))
                    nc.vector.tensor_scalar(cv[:, m, :], xs[:, m, 0:T], c["conv_w"][:, m, 0:1], c["conv_b"][:, m:m + 1],
                                            ALU.mult, ALU.add).then_inc(s["conv"], 1)
                    for j in range(1, DC):
                        dve.wait_ge(s["conv"], at(n + j))
                        nc.vector.scalar_tensor_tensor(out=cv[:, m, :], in0=xs[:, m, j:j + T], scalar=c["conv_w"][:, m, j:j + 1],
                                                       in1=cv[:, m, :], op0=ALU.mult, op1=ALU.add).then_inc(s["conv"], 1)
                for m in range(KI):
                    dve.wait_ge(s["w1_done"], at(KI * b + m + 1))
                    nc.vector.scalar_tensor_tensor(out=w1[:, m, :], in0=w1[:, m, :], scalar=-1.0, in1=ee[:, m, :],
                                                   op0=ALU.add, op1=ALU.subtract).then_inc(s["soft1"], 1)

        @block.gpsimd
        def _(pool):
            with pool.Fori(0, NB) as b:
                for m in range(KI):
                    n = KI * b + m
                    pool.wait_ge(s["soft1"], at(n + 1))
                    pool.wait_ge(s["ln_done"], at(n + 1))
                    nc.gpsimd.tensor_tensor(ln[:, m, :], ln[:, m, :], w1[:, m, :], ALU.subtract).then_inc(s["soft2"], 1)
                    pool.wait_ge(s["soft2"], at(n + 1))
                    nc.gpsimd.tensor_tensor(ab[:, m, :], ln[:, m, :], re[:, m, :], ALU.add).then_inc(s["dt_done"], 1)
                    pool.wait_ge(s["dt_done"], at(n + 1))
                    pool.wait_ge(s["uu_st"], at(16 * KI * b))
                    nc.gpsimd.tensor_tensor(uu[:, m, :], ab[:, m, :], U[:, m, :], ALU.mult).then_inc(s["uu_done"], 1)


def scan(nc, sb, pb, sem, counters, w, c, dram):
    DT, UU, U, Z = (sb(f"s_{n}", [P, KI, T]) for n in ("dt", "uu", "u", "z"))
    Bb = sb("s_B", [P, 2, SB, T])
    Cb = sb("s_C", [P, 2, SB, T])
    dA, uB, H = sb("s_dA", [P, DAR, GS, T]), sb("s_uB", [P, DAR, GS, T]), sb("s_H", [P, HR, GS, T])
    y2 = sb("s_y2", [P, 2, T])
    Y = [pb(f"s_Y{k}", [P, T]) for k in range(KI)]
    bc_in = [[sem(f"s_bc_in{i}{g}") for g in range(GPB)] for i in range(2)]
    du_in, z_in = [sem(f"s_du_in{k}") for k in range(KI)], [sem(f"s_z_in{k}") for k in range(KI)]
    y_st = [sem(f"s_y_st{i}") for i in range(2)]
    exp_done, uB_done, times_c = sem("s_exp_done"), sem("s_uB_done"), sem("s_times_c")
    scanned = sem("s_scanned")
    summed = sem("s_summed")
    gated = sem("s_gated")
    skip_in = sem("s_skip_in")

    def tile_of(d, b, k):
        return dram[d][bass.ds(b, 1), k * P:(k + 1) * P, :].rearrange("o p t -> p (o t)")

    def pairs(engine, b, body):
        with engine.Fori(0, NBLK // 2 - 1) as q:
            for i in range(2):
                body(b, 2 * q + i, i, False)
        for i in range(2):
            body(b, NBLK - 2 + i, i, i == 1)

    def group(b, blk, k, g):
        return GN * b + GB * blk + GPB * k + g

    begin(nc, counters)
    with nc.Block() as block:
        @block.sync
        def _(sp):
            def load_block(b, blk, i):
                for g in range(GPB):
                    for dst, lo in ((Bb, 0), (Cb, DS)):
                        src = dram["bc"][bass.ds(b, 1), bass.ds(lo + SB * blk + GS * g, GS), :].rearrange("o s t -> o (s t)")
                        sp.dma_start(dst[:, i, g * GS:(g + 1) * GS, :].rearrange("p s t -> p (s t)"),
                                     src.to_broadcast([P, GS * T])).then_inc(bc_in[i][g], 16)

            def load_du(b, k):
                for dst, name in ((DT, "dt"), (UU, "uu"), (U, "u")):
                    sp.dma_start(dst[:, k, :], tile_of(name, b, k)).then_inc(du_in[k], 16)

            load_block(0, 0, 0)
            for k in range(KI):
                load_du(0, k)

            def block_of(last_sequence):
                def body(b, blk, i, last):
                    sp.wait_ge(summed, at(GN * b + GB * blk))
                    if not last:
                        load_block(b, blk + 1, 1 - i)
                        return
                    if not last_sequence:
                        load_block(b + 1, 0, 1 - i)
                    for k in range(KI):
                        if not last_sequence:
                            sp.wait_ge(scanned, at(group(b, blk, k, GPB - 1) + 1))
                            load_du(b + 1, k)
                        sp.wait_ge(gated, at(KI * b + k + 1))
                        sp.dma_start(tile_of("y", b, k), y2[:, k % 2, :]).then_inc(y_st[k % 2], 16)
                return body

            def load_z(b):
                for k in range(KI):
                    sp.dma_start(Z[:, k, :], tile_of("z", b, k)).then_inc(z_in[k], 16)

            with sp.Fori(0, NB - 1) as b:
                load_z(b)
                pairs(sp, b, block_of(False))
            load_z(NB - 1)
            pairs(sp, NB - 1, block_of(True))
            for i in range(2):
                sp.wait_ge(y_st[i], at(16 * NB * KI // 2))

        @block.scalar
        def _(act):
            def body(b, blk, i, last):
                for k in range(KI):
                    act.wait_ge(du_in[k], at(48 * b + 48))
                    for g in range(GPB):
                        n = group(b, blk, k, g)
                        act.wait_ge(scanned, at(n + 1 - DAR))
                        for j in range(GS):
                            state = SB * blk + GS * g + j
                            last_ins = nc.scalar.activation(dA[:, g % DAR, j, :], DT[:, k, :], ACT.Exp,
                                                            scale=c["negA"][:, k, bass.ds(state, 1)])
                        last_ins.then_inc(exp_done, 1)
            with act.Fori(0, NB) as b:
                pairs(act, b, body)

        @block.vector
        def _(dve):
            def gate(b, k):
                dve.wait_ge(summed, at(group(b, NBLK - 1, k, GPB - 1) + 1))
                dve.wait_ge(z_in[k], at(16 * b + 16))
                dve.wait_ge(y_st[k % 2], at(16 * (2 * b + k // 2)))
                nc.vector.tensor_tensor(y2[:, k % 2, :], Y[k][:, :], Z[:, k, :], ALU.mult).then_inc(gated, 1)

            def body(b, blk, i, last):
                for k in range(KI):
                    dve.wait_ge(du_in[k], at(48 * b + 48))
                    for g in range(GPB):
                        n = group(b, blk, k, g)
                        uses = (b * (NBLK // 2) * 32 + ((blk - i) * 16 if not isinstance(blk, int) else (blk // 2) * 32)) + 32
                        dve.wait_ge(bc_in[i][g], at(uses))
                        dve.wait_ge(scanned, at(n + 1 - DAR))
                        nc.vector.tensor_tensor(uB[:, g % DAR], Bb[:, i, g * GS:(g + 1) * GS, :],
                                                UU[:, k:k + 1, :].to_broadcast([P, GS, T]), ALU.mult).then_inc(uB_done, 1)
                        dve.wait_ge(exp_done, at(n + 1))
                        dve.wait_ge(summed, at(n + 1 - HR))
                        dve.wait_ge(uB_done, at(n + 1))
                        for j in range(GS):
                            last_ins = nc.vector.tensor_tensor_scan(H[:, (GPB * k + g) % HR, j, :], dA[:, g % DAR, j, :],
                                                                    uB[:, g % DAR, j, :], 0.0, ALU.mult, ALU.add)
                        last_ins.then_inc(scanned, 1)
                    if last and k:
                        gate(b, k - 1)
                if last:
                    gate(b, KI - 1)
            with dve.Fori(0, NB) as b:
                pairs(dve, b, body)

        @block.gpsimd
        def _(pool):
            def body(b, blk, i, last):
                for k in range(KI):
                    for g in range(GPB):
                        n = group(b, blk, k, g)
                        pool.wait_ge(scanned, at(n + 1))
                        h = H[:, (GPB * k + g) % HR]
                        nc.gpsimd.tensor_tensor(h, h, Cb[:, i, g * GS:(g + 1) * GS, :], ALU.mult).then_inc(times_c, 1)
            with pool.Fori(0, NB) as b:
                pairs(pool, b, body)

        @block.tensor
        def _(pe):
            def body(b, blk, i, last):
                for k in range(KI):
                    for g in range(GPB):
                        n = group(b, blk, k, g)
                        pe.wait_ge(times_c, at(n + 1))
                        for j in range(GS):
                            last_ins = nc.tensor.matmul(Y[k][:, :], c["ident"][:, :], H[:, (GPB * k + g) % HR, j, :],
                                                        start=False, stop=(last and g == GPB - 1 and j == GS - 1))
                        last_ins.then_inc(summed, 1)
            with pe.Fori(0, NB) as b:
                for k in range(KI):
                    pe.wait_ge(du_in[k], at(48 * b + 48))
                    pe.wait_ge(gated, at(KI * b))
                    nc.tensor.matmul(Y[k][:, :], c["diagD"][:, k, :], U[:, k, :], start=True, stop=False).then_inc(skip_in, 1)
                pairs(pe, b, body)


def close(nc, sb, pb, sem, counters, w, c, dram):
    Yg, R = sb("c_y", [P, KI, T]), sb("c_r", [P, NJ, DM])
    x2, xn, O = sb("c_x2", [P, NJ, DM]), sb("c_xn", [P, NJ, DM]), sb("c_o", [P, NJ, DM])
    xnT = sb("c_xnT", [P, KM, T])
    st, mv, rs = sb("c_st", [P, NJ, 6]), sb("c_mv", [P, NJ, 2]), sb("c_rs", [P, NJ])
    sd = sb("c_sd", [P, NJ])
    pO = [pb(f"c_pO{i}", [P, 512]) for i in range(2)]
    pT = [pb(f"c_pT{i}", [P, KM, 256]) for i in range(2)]
    pF = [pb(f"c_pF{i}", [P, 512]) for i in range(2)]
    y_in, r_in, proj, x2_done, ln = sem("c_y_in"), sem("c_r_in"), sem("c_proj"), sem("c_x2_done"), sem("c_ln")
    n1, t1, t1_out, ffn, o_done, o_st = sem("c_n1"), sem("c_t1"), sem("c_t1_out"), sem("c_ffn"), sem("c_o_done"), sem("c_o_st")
    rt = sem("c_rt")

    begin(nc, counters)
    with nc.Block() as block:
        @block.sync
        def _(sp):
            def load(b):
                sp.wait_ge(proj, at(NJ * b))
                sp.dma_start(Yg[:, :, :], dram["y"][bass.ds(b, 1)].rearrange("o (k p) t -> p (o k) t", p=P)).then_inc(y_in, 16)
                sp.wait_ge(x2_done, at(NJ * b))
                sp.dma_start(R[:, :, :], dram["r"][bass.ds(b, 1)].rearrange("o (j p) d -> p (o j) d", p=P)).then_inc(r_in, 16)

            def store(b):
                sp.wait_ge(o_done, at(NJ * b + NJ))
                sp.dma_start(dram["out"][bass.ds(b, 1)].rearrange("o (j p) d -> p (o j) d", p=P), O[:, :, :]).then_inc(o_st, 16)
            load(0)
            with sp.Fori(0, NB - 1) as b:
                load(b + 1)
                store(b)
            store(NB - 1)
            sp.wait_ge(o_st, at(16 * NB))

        @block.tensor
        def _(pe):
            with pe.Fori(0, NB) as b:
                pe.wait_ge(y_in, at(16 * b + 16))
                for j in range(NJ):
                    pe.wait_ge(x2_done, at(NJ * b + (j - 1 if j > 1 else 0)))
                    for k in range(KI):
                        last = nc.tensor.matmul(pO[j % 2][:, 0:DM], Yg[:, k, j * P:(j + 1) * P], c["Wout"][:, k, :],
                                                start=(k == 0), stop=(k == KI - 1))
                    last.then_inc(proj, 1)
                for j in range(NJ + 1):
                    if j < NJ:
                        pe.wait_ge(n1, at(NJ * b + j + 1))
                        pe.wait_ge(t1_out, at(KM * (NJ * b + (j - 1 if j > 1 else 0))))
                        for k in range(KM):
                            last = nc.tensor.transpose(pT[j % 2][:, k, 0:P], xn[:, j, k * P:(k + 1) * P], c["ident"][:, :])
                        last.then_inc(t1, 1)
                    if j:
                        i = j - 1
                        pe.wait_ge(t1_out, at(KM * (NJ * b + i + 1)))
                        pe.wait_ge(o_done, at(NJ * b + (i - 1 if i > 1 else 0)))
                        nc.tensor.matmul(pF[i % 2][:, 0:DM], c["ones"][:, :], c["bias"][:, :], start=True, stop=False)
                        for k in range(KM):
                            last = nc.tensor.matmul(pF[i % 2][:, 0:DM], xnT[:, k, i * P:(i + 1) * P], c["Wf"][:, k, :],
                                                    start=False, stop=(k == KM - 1))
                        last.then_inc(ffn, 1)

        @block.scalar
        def _(act):
            with act.Fori(0, NB) as b:
                deviation(nc, act, ln, rt, mv, sd, 3 * b)
                act.wait_ge(ffn, at(NJ * b))
                for j in range(NJ):
                    act.wait_ge(t1, at(NJ * b + j + 1))
                    for k in range(KM):
                        nc.scalar.activation(xnT[:, k, j * P:(j + 1) * P], pT[j % 2][:, k, 0:P], ACT.Copy).then_inc(t1_out, 1)

        @block.vector
        def _(dve):
            with dve.Fori(0, NB) as b:
                dve.wait_ge(r_in, at(16 * b + 16))
                dve.wait_ge(o_done, at(NJ * b))
                for j in range(NJ):
                    dve.wait_ge(proj, at(NJ * b + j + 1))
                    nc.vector.tensor_tensor(x2[:, j, :], R[:, j, :], pO[j % 2][:, 0:DM], ALU.add).then_inc(x2_done, 1)
                dve.wait_ge(x2_done, at(NJ * b + NJ))
                dve.wait_ge(t1, at(NJ * b))
                dve.wait_ge(n1, at(NJ * b))
                layer_norm(nc, dve, ln, rt, x2, xn, st, mv, sd, rs, n1, 3 * b, b)
                dve.wait_ge(o_st, at(16 * b))
                for j in range(NJ):
                    dve.wait_ge(ffn, at(NJ * b + j + 1))
                    nc.vector.tensor_tensor(O[:, j, :], x2[:, j, :], pF[j % 2][:, 0:DM], ALU.add).then_inc(o_done, 1)


def macaron(nc, w, out):
    dram = {"x": w["x"], "out": out}
    for name, shape in (("r", [NB, T, DM]), ("hT", [NB, KM, P, T]), ("u", [NB, DI, T]), ("z", [NB, DI, T]), ("dt", [NB, DI, T]),
                        ("uu", [NB, DI, T]), ("bc", [NB, 2 * DS, T]), ("y", [NB, DI, T])):
        dram[name] = nc.dram_tensor("scratch_" + name, shape, fp32).ap()

    def run(stage):
        with ExitStack() as own:
            counters = []
            sb, pb, sem = tools(nc, own, counters)
            stage(nc, sb, pb, sem, counters, w, c, dram)

    with ExitStack() as ctx:
        sb, _, _ = tools(nc, ctx)
        c = {n: sb("w_" + n, s) for n, s in (
            ("ident", [P, P]), ("diagD", [P, KI, P]), ("negA", [P, KI, DS]), ("Wf", [P, KM, DM]), ("bias", [1, DM]), ("ones", [1, P]),
            ("conv_w", [P, KI, DC]), ("conv_b", [P, KI]), ("dt_b", [P, KI]), ("D", [P, KI]), ("norm_w", [P, KM]), ("norm_b", [P, KM]),
            ("Wout", [P, KI, DM]))}
        with ExitStack() as early:
            esb, _, _ = tools(nc, early)
            c["Win"], c["dt_w"], c["bc_w"] = esb("w_Win", [P, KM, 2 * DI]), esb("w_dt", [P, KI, DI]), esb("w_bc", [P, KI, 2 * DS])
            with ExitStack() as own:
                constants(nc, *tools(nc, own), w, c)
            run(first_ffn)
            run(projections)
        run(scan)
        run(close)


def kernel(**inputs):
    import numpy as np
    import concourse.bacc as bacc
    from concourse.bass_utils import run_bass_kernel_spmd

    given = {n.split("_", 2)[2] if not n.endswith("kernel") else "kernel": np.asarray(a) for n, a in inputs.items()}
    given["aT"] = given.pop("a").T
    nc = bacc.Bacc("TRN2", target_bir_lowering=False, num_devices=1)
    arrays, w = {}, {}
    for n, a in given.items():
        arrays["in_" + n] = np.ascontiguousarray(a)
        w[n] = nc.dram_tensor("in_" + n, a.shape, mybir.dt.from_np(a.dtype), kind="ExternalInput").ap()
    out = nc.dram_tensor("out", (NB, T, DM), fp32, kind="ExternalOutput").ap()
    macaron(nc, w, out)
    r = run_bass_kernel_spmd(nc, [arrays], core_ids=[0])
    return r.results[0]["out"]
```

```python
from contextlib import ExitStack

import concourse.bass as bass
from concourse import mybir

P = 128
NB, T, DM = 16, 512, 256
DI, DS, DC = 512, 64, 4
RANK = 16
EPS = 1e-5
QMAX = 7.0
ROUND = 12582912.0
KM, KI, NJ = DM // P, DI // P, T // P
GS = 4
NBLK = DS // GS
GN = NBLK * KI
START = 16
DAR, HR = 2, 4
PAIR = NJ // 2

fp32 = mybir.dt.float32
ALU = mybir.AluOpType
ACT = mybir.ActivationFunctionType
AX = mybir.AxisListType


def at(n):
    return START + n


def begin(nc, counters):
    with nc.Block() as block:
        @block.sync
        def _(sp):
            for s in counters:
                sp.sem_inc(s, START)


def tools(nc, ctx, counters=None):
    def sb(name, shape, dt=fp32):
        return ctx.enter_context(nc.sbuf_tensor(name, shape, dt))

    def pb(name, shape, dt=fp32):
        return ctx.enter_context(nc.psum_tensor(name, shape, dt))

    def sem(name):
        s = ctx.enter_context(nc.semaphore(name))
        if counters is not None:
            counters.append(s)
        return s

    return sb, pb, sem


def constants(nc, sb, pb, sem, w, c):
    wk, aT, lb = sb("wk", [P, KM, DM]), sb("aT", [RANK, DM]), sb("lb", [RANK, DM])
    wabs, wq = sb("wabs", [P, KM, DM]), sb("wq", [P, KM, DM])
    mx, mx1, one, sc, alog = sb("mx", [P, 1]), sb("mx1", [1, 1]), sb("one", [1, P]), sb("sc", [P, 4]), sb("alog", [P, KI, DS])
    biasr = sb("biasr", [1, DM])
    pm, pab = pb("pm", [P, 512]), pb("pab", [P, KM, DM])
    k_small, k_big, k_id, k_abs, k_chain = sem("k_small"), sem("k_big"), sem("k_id"), sem("k_abs"), sem("k_chain")
    k_row, k_col, k_ab, k_one, k_expA, k_d = sem("k_row"), sem("k_col"), sem("k_ab"), sem("k_one"), sem("k_expA"), sem("k_d")

    with nc.Block() as block:
        @block.sync
        def _(sp):
            small = [(wk[:, :, :], w["kernel"].rearrange("(k p) f -> p k f", p=P)), (aT[:, :], w["aT"]), (lb[:, :], w["b"]),
                     (biasr[:, :], w["bias"].rearrange("(o f) -> o f", o=1)),
                     (alog[:, :, :], w["A_log"].rearrange("(k p) s -> p k s", p=P)),
                     (c["conv_w"][:, :, :], w["conv_w"].rearrange("(k p) o j -> p k (o j)", p=P))]
            small += [(c[n][:, :], w[n].rearrange("(k p) -> p k", p=P)) for n in ("conv_b", "dt_b", "D", "norm_w", "norm_b")]
            with nc.allow_non_contiguous_dma(reason="a few KiB, once"):
                for dst, src in small:
                    sp.dma_start(dst, src).then_inc(k_small, 16)
            for dst, src in ((c["Win"][:, :, :], w["Win"].rearrange("(k p) m -> p k m", p=P)),
                             (c["dt_w"][:, :, :], w["dt_w"].rearrange("(k p) m -> p k m", p=P)),
                             (c["bc_w"][:, :, 0:DS], w["Bp"].rearrange("(k p) m -> p k m", p=P)),
                             (c["bc_w"][:, :, DS:2 * DS], w["Cp"].rearrange("(k p) m -> p k m", p=P)),
                             (c["Wout"][:, :, :], w["Wout"].rearrange("(k p) m -> p k m", p=P))):
                sp.dma_start(dst, src).then_inc(k_big, 16)
            sp.wait_ge(k_big, 5 * 16)
            sp.wait_ge(k_small, 11 * 16)

        @block.gpsimd
        def _(pool):
            nc.gpsimd.memset(c["ident"][:, :], 0.0).then_inc(k_id, 1)
            pool.wait_ge(k_id, 1)
            nc.gpsimd.affine_select(out=c["ident"][:, :], in_=c["ident"][:, :], compare_op=ALU.not_equal, fill=1.0,
                                    base=0, pattern=[[-1, P]], channel_multiplier=1).then_inc(k_id, 1)

        @block.scalar
        def _(act):
            act.wait_ge(k_small, 11 * 16)
            nc.scalar.activation(wabs[:, :, :], wk[:, :, :], ACT.Abs).then_inc(k_abs, 1)
            nc.scalar.activation(c["negA"][:, :, :], alog[:, :, :], ACT.Exp).then_inc(k_expA, 1)

        @block.tensor
        def _(pe):
            pe.wait_ge(k_id, 2)
            pe.wait_ge(k_chain, 1)
            nc.tensor.matmul(pm[0:1, 0:P], mx[:, :], c["ident"][:, :], start=True, stop=True).then_inc(k_row, 1)
            pe.wait_ge(k_one, 1)
            pe.wait_ge(k_chain, 2)
            nc.tensor.matmul(pm[:, P:P + 1], one[:, :], mx1[:, :], start=True, stop=True).then_inc(k_col, 1)
            pe.wait_ge(k_small, 11 * 16)
            for k in range(KM):
                nc.tensor.matmul(pab[:, k, :], aT[:, k * P:(k + 1) * P], lb[:, :], start=(k == 0), stop=(k == KM - 1),
                                 skip_group_check=True).then_inc(k_ab, 1)

        @block.vector
        def _(dve):
            n = [0]

            def link(ins):
                n[0] += 1
                ins.then_inc(k_chain, 1)
                dve.wait_ge(k_chain, n[0])

            nc.vector.memset(one[:, :], 1.0).then_inc(k_one, 1)
            dve.wait_ge(k_abs, 1)
            link(nc.vector.reduce_max(mx[:, :], wabs[:, :, :].rearrange("p k f -> p (k f)"), AX.X))
            dve.wait_ge(k_row, 1)
            link(nc.vector.reduce_max(mx1[:, :], pm[0:1, 0:P], AX.X))
            dve.wait_ge(k_col, 1)
            link(nc.vector.tensor_scalar(sc[:, 0:1], pm[:, P:P + 1], 1.0 / QMAX, None, ALU.mult))
            link(nc.vector.reciprocal(sc[:, 1:2], sc[:, 0:1]))
            link(nc.vector.tensor_scalar(sc[:, 2:3], sc[:, 0:1], 0.5, None, ALU.mult))
            link(nc.vector.tensor_scalar(wq[:, :, :], wk[:, :, :], sc[:, 1:2], ROUND, ALU.mult, ALU.add))
            link(nc.vector.tensor_scalar(wabs[:, :, :], wq[:, :, :], ROUND, QMAX, ALU.subtract, ALU.min))
            link(nc.vector.tensor_scalar(wq[:, :, :], wabs[:, :, :], -8.0, sc[:, 2:3], ALU.max, ALU.mult))
            dve.wait_ge(k_ab, KM)
            link(nc.vector.scalar_tensor_tensor(out=c["Wf"][:, :, :], in0=pab[:, :, :], scalar=0.5, in1=wq[:, :, :],
                                                op0=ALU.mult, op1=ALU.add))
            dve.wait_ge(k_small, 11 * 16)
            link(nc.vector.tensor_scalar(c["bias"][:, :], biasr[:, :], 0.5, None, ALU.mult))
            link(nc.vector.tensor_copy(c["ones"][:, :], one[:, :]))
            dve.wait_ge(k_expA, 1)
            link(nc.vector.tensor_scalar(c["negA"][:, :, :], c["negA"][:, :, :], -1.0, None, ALU.mult))
            dve.wait_ge(k_id, 2)
            for k in range(KI):
                nc.vector.tensor_scalar(c["diagD"][:, k, :], c["ident"][:, :], c["D"][:, k:k + 1], None, ALU.mult).then_inc(k_d, 1)


def moments(nc, dve, tag, xs, st, mv, rs, count):
    for j in range(NJ):
        last = nc.vector.bn_stats(st[:, j, :], xs[:, j, :])
    last.then_inc(tag, 1)
    dve.wait_ge(tag, at(count + 1))
    nc.vector.memset(rs[:, :], 0.0)
    for j in range(NJ):
        last = nc.vector.bn_aggr(mv[:, j, :], st[:, j, :])
    last.then_inc(tag, 1)


def deviation(nc, act, tag, root, mv, sd, count):
    act.wait_ge(tag, at(count + 2))
    nc.scalar.activation(sd[:, :], mv[:, :, 1], ACT.Sqrt, bias=EPS).then_inc(root, 1)


def normalize(nc, dve, tag, root, xs, out, mv, sd, rs, done, count, seq):
    dve.wait_ge(root, at(seq + 1))
    nc.vector.reciprocal(rs[:, :], sd[:, :]).then_inc(tag, 1)
    dve.wait_ge(tag, at(count + 3))
    for j in range(NJ):
        last = nc.vector.tensor_scalar(out[:, j, :], xs[:, j, :], mv[:, j, 0:1], rs[:, j:j + 1], ALU.subtract, ALU.mult)
    last.then_inc(done, 1)


def layers(nc, sb, pb, sem, counters, c, dram):
    X, X1, XA = sb("X", [P, NJ, DM]), sb("X1", [P, NJ, DM]), sb("XA", [P, NJ, DM])
    RL, X2 = sb("RL", [P, NJ, DM]), sb("X2", [P, NJ, DM])
    XN, XNT = sb("XN", [P, NJ, DM]), sb("XNT", [P, KM, T])
    st, mv, sd, rs = sb("st", [P, NJ, 6]), sb("mv", [P, NJ, 2]), sb("sd", [P, NJ]), sb("rs", [P, NJ])
    cst, cmv, csd, crs = sb("cst", [P, NJ, 6]), sb("cmv", [P, NJ, 2]), sb("csd", [P, NJ]), sb("crs", [P, NJ])
    hT, U = sb("hT", [P, KM, T]), sb("U", [P, KI, T])
    xs = sb("xs", [P, 2, DC - 1 + T])
    cv, zo, BC = sb("cv", [P, 2, T]), sb("zo", [P, 2, T]), sb("BC", [P, T])
    absv, ev, lnv, ev1, relu = (sb(n, [P, T]) for n in ("absv", "ev", "lnv", "ev1", "relu"))
    dto, duo = sb("dto", [P, T]), sb("duo", [P, T])
    DT, DU, ZL = sb("DT", [P, KI, T]), sb("DU", [P, KI, T]), sb("ZL", [P, 2, T])
    Bb, Cb = sb("Bb", [P, 2, GS, T]), sb("Cb", [P, 2, GS, T])
    dA, H = sb("dA", [P, DAR, GS, T]), sb("H", [P, HR, GS, T])
    YG = sb("YG", [P, KI, T])
    Y = [pb(f"Y{k}", [P, T]) for k in range(KI)]
    pP = [pb(f"pP{i}", [P, T]) for i in range(2)]
    pA = [pb(f"pA{i}", [P, 2, DM]) for i in range(2)]

    x_in, x1_done, r_done, r_st, h_out = sem("x_in"), sem("x1_done"), sem("r_done"), sem("r_st"), sem("h_out")
    ln1, ln2, ln3, root1, root2, root3, n1, n2, n3 = (sem(n) for n in ("ln1", "ln2", "ln3", "root1", "root2", "root3", "n1", "n2", "n3"))
    t1, t1_out, ffn1, t2 = sem("t1"), sem("t1_out"), sem("ffn1"), sem("t2")
    r_in, y_mm, x2_done, lnc, rootc, nc_done = sem("r_in"), sem("y_mm"), sem("x2_done"), sem("lnc"), sem("rootc"), sem("nc_done")
    tc, tc_out, ffnc, o_done, o_st = sem("tc"), sem("tc_out"), sem("ffnc"), sem("o_done"), sem("o_st")
    zero, mm_x, mm_z, mm_bc, mm_dt = sem("zero"), sem("mm_x"), sem("mm_z"), sem("mm_bc"), sem("mm_dt")
    xs_out, conv, u_done, z_done, bc_out = sem("xs_out"), sem("conv"), sem("u_done"), sem("z_done"), sem("bc_out")
    abs_done, relu_done, exp_done, ln_done, one_done = sem("abs_done"), sem("relu_done"), sem("exp_done"), sem("ln_done"), sem("one_done")
    soft1, soft2, dt_done, du_done = sem("soft1"), sem("soft2"), sem("dt_done"), sem("du_done")
    z_st, bc_st, dt_st, du_st = [sem(f"z_st{i}") for i in range(2)], sem("bc_st"), sem("dt_st"), sem("du_st")
    z_in, du_in = [sem(f"z_in{i}") for i in range(2)], [sem(f"du_in{k}") for k in range(KI)]
    bc_in = [sem(f"bc_in{i}") for i in range(2)]
    decay, forced, scanned, times_c, summed, skip, gated = (sem(n) for n in ("decay", "forced", "scanned", "times_c", "summed", "skip", "gated"))

    def tile_of(d, b, k):
        return dram[d][bass.ds(b, 1), k * P:(k + 1) * P, :].rearrange("o p t -> p (o t)")

    def tokens_of(d, b):
        return dram[d][bass.ds(b, 1)].rearrange("o (j p) d -> p (o j) d", p=P)

    def ffns(b):
        return min(b + 2, NB) if isinstance(b, int) else b + 2

    def steps(engine, step):
        step(-2, False, False, False, True)
        step(-1, False, False, True, True)
        step(0, True, False, True, True)
        with engine.Fori(1, NB - 2) as b:
            step(b, True, True, True, True)
        step(NB - 2, True, True, True, False)
        step(NB - 1, True, True, False, False)
        step(NB, False, True, False, False)

    begin(nc, counters)
    with nc.Block() as block:
        @block.sync
        def _(sp):
            def load_block(b, blk):
                for dst, lo in ((Bb, 0), (Cb, DS)):
                    src = dram["bc"][bass.ds(b, 1), lo + GS * blk:lo + GS * (blk + 1), :].rearrange("o s t -> o (s t)")
                    sp.dma_start(dst[:, blk % 2].rearrange("p s t -> p (s t)"), src.to_broadcast([P, GS * T])).then_inc(bc_in[blk % 2], 16)

            def load_z(b, k):
                sp.wait_ge(gated, at(KI * b + k - 1))
                sp.wait_ge(z_st[k % 2], at(16 * (2 * b + k // 2 + 1)))
                sp.dma_start(ZL[:, k % 2, :], tile_of("z", b, k)).then_inc(z_in[k % 2], 16)

            def load_du(b, k):
                sp.wait_ge(scanned, at(GN * b - KI + k + 1))
                sp.wait_ge(dt_st, at(16 * (KI * b + k + 1)))
                sp.wait_ge(du_st, at(16 * (KI * b + k + 1)))
                sp.dma_start(DT[:, k, :], tile_of("dt", b, k)).then_inc(du_in[k], 16)
                sp.dma_start(DU[:, k, :], tile_of("du", b, k)).then_inc(du_in[k], 16)

            def store_z(q, m):
                sp.wait_ge(z_done, at(KI * q + m + 1))
                sp.dma_start(tile_of("z", q, m), zo[:, m % 2, :]).then_inc(z_st[m % 2], 16)

            def store_du(q, m):
                sp.wait_ge(dt_done, at(KI * q + m + 1))
                sp.dma_start(tile_of("dt", q, m), dto[:, :]).then_inc(dt_st, 16)
                sp.wait_ge(du_done, at(KI * q + m + 1))
                sp.dma_start(tile_of("du", q, m), duo[:, :]).then_inc(du_st, 16)

            def step(b, scan, close, proj, ffn):
                c_, q, a = b - 1, b + 1, b + 2
                for n in range(GN):
                    blk, k = n // KI, n % KI
                    if scan and k == 0 and blk < NBLK - 1:
                        sp.wait_ge(summed, at(GN * b + n))
                        load_block(b, blk + 1)
                    if close and n < 2:
                        load_z(c_, 2 + n)
                    if close and n == 2:
                        sp.wait_ge(x2_done, at(2 * c_))
                        sp.wait_ge(r_st, at(16 * c_ + 16))
                        sp.dma_start(RL[:, :, :], tokens_of("r", c_)).then_inc(r_in, 16)
                    if proj and n in (20, 26):
                        store_z(q, 0 if n == 20 else 2)
                        store_z(q, 1 if n == 20 else 3)
                    if ffn and n == 24:
                        sp.wait_ge(x1_done, at(2 * a))
                        sp.dma_start(X[:, :, :], tokens_of("x", a)).then_inc(x_in, 16)
                    if scan and n in (28, 29):
                        load_z(b, n - 28)
                    if close and n == 31:
                        sp.wait_ge(o_done, at(2 * c_ + 2))
                        sp.dma_start(tokens_of("out", c_), X2[:, :, :]).then_inc(o_st, 16)
                    if proj and n == 32:
                        sp.wait_ge(bc_out, at(q + 1))
                        sp.dma_start(dram["bc"][bass.ds(q, 1)].rearrange("o p t -> p (o t)"), BC[:, :]).then_inc(bc_st, 16)
                    if proj and n in (36, 42, 48, 54):
                        store_du(q, (n - 36) // 6)
                    if ffn and n == 56:
                        sp.wait_ge(r_done, at(a + 1))
                        sp.dma_start(tokens_of("r", a), X1[:, :, :]).then_inc(r_st, 16)
                    if proj and n == GN - KI:
                        sp.wait_ge(summed, at(GN * q - KI))
                        sp.wait_ge(bc_st, at(16 * q + 16))
                        load_block(q, 0)
                    if proj and n >= GN - KI:
                        load_du(q, k)

            steps(sp, step)
            sp.wait_ge(o_st, at(16 * NB))

        @block.scalar
        def _(act):
            def take_xs(q, m):
                act.wait_ge(mm_x, at(KI * q + m + 1))
                act.wait_ge(conv, at(DC * (KI * q + m - 1)))
                nc.scalar.activation(xs[:, m % 2, DC - 1:], pP[m % 2][:, :], ACT.Copy).then_inc(xs_out, 1)

            def silu_u(q, m):
                act.wait_ge(conv, at(DC * (KI * q + m + 1)))
                act.wait_ge(mm_dt, at(KI * q))
                act.wait_ge(du_done, at(KI * q))
                act.wait_ge(skip, at(KI * q))
                nc.scalar.activation(U[:, m, :], cv[:, m % 2, :], ACT.Silu).then_inc(u_done, 1)

            def silu_z(q, m):
                act.wait_ge(mm_z, at(KI * q + m + 1))
                act.wait_ge(z_st[m % 2], at(16 * (2 * q + m // 2)))
                nc.scalar.activation(zo[:, m % 2, :], pP[m % 2][:, :], ACT.Silu).then_inc(z_done, 1)

            def softplus(q, m):
                n = KI * q + m
                v = pP[(m + 1) % 2][:, :]
                act.wait_ge(mm_dt, at(n + 1))
                act.wait_ge(dt_done, at(n))
                act.wait_ge(exp_done, at(n))
                nc.scalar.activation(absv[:, :], v, ACT.Abs, bias=c["dt_b"][:, m:m + 1]).then_inc(abs_done, 1)
                nc.scalar.activation(relu[:, :], v, ACT.Relu, bias=c["dt_b"][:, m:m + 1]).then_inc(relu_done, 1)
                act.wait_ge(abs_done, at(n + 1))
                nc.scalar.activation(ev[:, :], absv[:, :], ACT.Exp, scale=-1.0).then_inc(exp_done, 1)
                act.wait_ge(exp_done, at(n + 1))
                nc.scalar.activation(lnv[:, :], ev[:, :], ACT.Ln, bias=1.0).then_inc(ln_done, 1)
                nc.scalar.activation(ev1[:, :], ev[:, :], ACT.Copy, bias=1.0).then_inc(one_done, 1)

            def step(b, scan, close, proj, ffn):
                c_, q, a = b - 1, b + 1, b + 2
                for n in range(GN):
                    blk, k = n // KI, n % KI
                    if scan:
                        if blk == 0:
                            act.wait_ge(du_in[k], at(32 * b + 32))
                        act.wait_ge(scanned, at(GN * b + n + 1 - DAR))
                        for j in range(GS):
                            last = nc.scalar.activation(dA[:, n % DAR, j, :], DT[:, k, :], ACT.Exp,
                                                        scale=c["negA"][:, k, GS * blk + j:GS * blk + j + 1])
                        last.then_inc(decay, 1)
                    if proj and n in (5, 6):
                        take_xs(q, n - 5)
                    if proj and n == 12:
                        take_xs(q, 2)
                        silu_u(q, 0)
                        silu_u(q, 1)
                    if proj and n == 13:
                        take_xs(q, 3)
                    if close and n == 14:
                        deviation(nc, act, lnc, rootc, cmv, csd, 3 * c_)
                    if proj and n == 19:
                        silu_u(q, 2)
                        silu_u(q, 3)
                        silu_z(q, 0)
                        silu_z(q, 1)
                    if close and n in (22, 23):
                        i = n - 22
                        act.wait_ge(tc, at(2 * c_ + i + 1))
                        nc.scalar.activation(XNT[:, :, i * PAIR * P:(i + 1) * PAIR * P], pA[i][:, :, :], ACT.Copy).then_inc(tc_out, 1)
                    if proj and n == 25:
                        silu_z(q, 2)
                        silu_z(q, 3)
                    if proj and n == 30:
                        act.wait_ge(mm_bc, at(q + 1))
                        act.wait_ge(bc_st, at(16 * q))
                        nc.scalar.activation(BC[:, :], pP[0][:, :], ACT.Copy).then_inc(bc_out, 1)
                    if proj and n in (32, 38, 44, 50):
                        softplus(q, (n - 32) // 6)
                    if ffn and n == 33:
                        deviation(nc, act, ln1, root1, mv, sd, 3 * a)
                    if ffn and n in (40, 41):
                        i = n - 40
                        act.wait_ge(t1, at(2 * a + i + 1))
                        nc.scalar.activation(XNT[:, :, i * PAIR * P:(i + 1) * PAIR * P], pA[i][:, :, :], ACT.Copy).then_inc(t1_out, 1)
                    if ffn and n == 51:
                        deviation(nc, act, ln2, root2, mv, sd, 3 * a)
                    if ffn and n == 56:
                        deviation(nc, act, ln3, root3, mv, sd, 3 * a)
                    if ffn and n in (62, 63):
                        i = n - 62
                        act.wait_ge(t2, at(2 * a + i + 1))
                        for k_ in range(KM):
                            last = nc.scalar.activation(hT[:, k_, i * PAIR * P:(i + 1) * PAIR * P], pA[i][:, k_, :], ACT.Identity,
                                                        scale=c["norm_w"][:, k_:k_ + 1], bias=c["norm_b"][:, k_:k_ + 1])
                        last.then_inc(h_out, 1)

            act.wait_ge(zero, at(1))
            steps(act, step)

        @block.vector
        def _(dve):
            def conv4(q, m):
                n = KI * q + m
                dve.wait_ge(xs_out, at(n + 1))
                dve.wait_ge(u_done, at(n - 1))
                x, y = xs[:, m % 2], cv[:, m % 2, :]
                nc.vector.tensor_scalar(y, x[:, 0:T], c["conv_w"][:, m, 0:1], c["conv_b"][:, m:m + 1], ALU.mult, ALU.add).then_inc(conv, 1)
                for j in range(1, DC):
                    dve.wait_ge(conv, at(DC * n + j))
                    nc.vector.scalar_tensor_tensor(out=y, in0=x[:, j:j + T], scalar=c["conv_w"][:, m, j:j + 1], in1=y,
                                                   op0=ALU.mult, op1=ALU.add).then_inc(conv, 1)

            def step(b, scan, close, proj, ffn):
                c_, q, a = b - 1, b + 1, b + 2
                for n in range(GN):
                    blk, k = n // KI, n % KI
                    if close and blk == 0:
                        dve.wait_ge(summed, at(GN * c_ + GN - KI + k + 1))
                        dve.wait_ge(z_in[k % 2], at(16 * (2 * c_ + k // 2 + 1)))
                        dve.wait_ge(y_mm, at(2 * c_))
                        nc.vector.tensor_tensor(YG[:, k, :], Y[k][:, :], ZL[:, k % 2, :], ALU.mult).then_inc(gated, 1)
                    if scan:
                        h = H[:, n % HR]
                        if blk == 0:
                            dve.wait_ge(du_in[k], at(32 * b + 32))
                        if k == 0:
                            dve.wait_ge(bc_in[blk % 2], at(32 * (b * (NBLK // 2) + blk // 2 + 1)))
                        dve.wait_ge(summed, at(GN * b + n + 1 - HR))
                        nc.vector.tensor_tensor(h, Bb[:, blk % 2], DU[:, k:k + 1, :].to_broadcast([P, GS, T]), ALU.mult).then_inc(forced, 1)
                        dve.wait_ge(decay, at(GN * b + n + 1))
                        dve.wait_ge(forced, at(GN * b + n + 1))
                        for j in range(GS):
                            last = nc.vector.tensor_tensor_scan(h[:, j, :], dA[:, n % DAR, j, :], h[:, j, :], 0.0, ALU.mult, ALU.add)
                        last.then_inc(scanned, 1)
                    if proj and n in (7, 8, 14, 15):
                        conv4(q, (7, 8, 14, 15).index(n))
                    if close and n in (9, 10):
                        i = n - 9
                        dve.wait_ge(r_in, at(16 * c_ + 16))
                        dve.wait_ge(y_mm, at(2 * c_ + i + 1))
                        dve.wait_ge(o_st, at(16 * c_))
                        nc.vector.tensor_tensor(X2[:, 2 * i:2 * i + 2, :], RL[:, 2 * i:2 * i + 2, :], pA[i][:, :, :], ALU.add).then_inc(x2_done, 1)
                    if close and n == 11:
                        dve.wait_ge(x2_done, at(2 * c_ + 2))
                        dve.wait_ge(nc_done, at(c_))
                        moments(nc, dve, lnc, X2, cst, cmv, crs, 3 * c_)
                    if close and n == 16:
                        dve.wait_ge(t2, at(2 * ffns(b)))
                        normalize(nc, dve, lnc, rootc, X2, XN, cmv, csd, crs, nc_done, 3 * c_, c_)
                    if close and n in (28, 29):
                        i = n - 28
                        dve.wait_ge(ffnc, at(2 * c_ + i + 1))
                        nc.vector.tensor_tensor(X2[:, 2 * i:2 * i + 2, :], X2[:, 2 * i:2 * i + 2, :], pA[i][:, :, :], ALU.add).then_inc(o_done, 1)
                    if ffn and n == 30:
                        dve.wait_ge(x_in, at(16 * a + 16))
                        dve.wait_ge(n3, at(a))
                        moments(nc, dve, ln1, X, st, mv, rs, 3 * a)
                    if proj and n in (33, 39, 45, 51):
                        m = KI * q + (n - 33) // 6
                        dve.wait_ge(one_done, at(m + 1))
                        nc.vector.scalar_tensor_tensor(out=ev1[:, :], in0=ev1[:, :], scalar=-1.0, in1=ev[:, :],
                                                       op0=ALU.add, op1=ALU.subtract).then_inc(soft1, 1)
                    if ffn and n == 34:
                        dve.wait_ge(tc, at(2 * a - 4))
                        dve.wait_ge(t2, at(2 * a))
                        normalize(nc, dve, ln1, root1, X, XN, mv, sd, rs, n1, 3 * a, a)
                    if ffn and n in (46, 47):
                        i = n - 46
                        dve.wait_ge(ffn1, at(2 * a + i + 1))
                        dve.wait_ge(r_st, at(16 * a))
                        nc.vector.tensor_tensor(X1[:, 2 * i:2 * i + 2, :], X[:, 2 * i:2 * i + 2, :], pA[i][:, :, :], ALU.add).then_inc(x1_done, 1)
                    if ffn and n == 48:
                        dve.wait_ge(x1_done, at(2 * a + 2))
                        dve.wait_ge(n1, at(a + 1))
                        moments(nc, dve, ln2, X1, st, mv, rs, 3 * a)
                    if ffn and n == 52:
                        dve.wait_ge(r_done, at(a))
                        normalize(nc, dve, ln2, root2, X1, XA, mv, sd, rs, n2, 3 * a, a)
                    if ffn and n == 53:
                        dve.wait_ge(n2, at(a + 1))
                        moments(nc, dve, ln3, XA, st, mv, rs, 3 * a)
                    if ffn and n == 57:
                        dve.wait_ge(t1, at(2 * a + 2))
                        normalize(nc, dve, ln3, root3, XA, XN, mv, sd, rs, n3, 3 * a, a)

            nc.vector.memset(xs[:, :, 0:DC - 1], 0.0).then_inc(zero, 1)
            dve.wait_ge(zero, at(1))
            steps(dve, step)

        @block.gpsimd
        def _(pool):
            def step(b, scan, close, proj, ffn):
                q, a = b + 1, b + 2
                for n in range(GN):
                    blk, h = n // KI, H[:, n % HR]
                    if scan:
                        pool.wait_ge(scanned, at(GN * b + n + 1))
                        nc.gpsimd.tensor_tensor(h, h, Cb[:, blk % 2], ALU.mult).then_inc(times_c, 1)
                    if proj and n in (34, 40, 46, 52):
                        m = (n - 34) // 6
                        s = KI * q + m
                        pool.wait_ge(soft1, at(s + 1))
                        pool.wait_ge(ln_done, at(s + 1))
                        nc.gpsimd.tensor_tensor(lnv[:, :], lnv[:, :], ev1[:, :], ALU.subtract).then_inc(soft2, 1)
                        pool.wait_ge(soft2, at(s + 1))
                        pool.wait_ge(relu_done, at(s + 1))
                        pool.wait_ge(dt_st, at(16 * s))
                        nc.gpsimd.tensor_tensor(dto[:, :], lnv[:, :], relu[:, :], ALU.add).then_inc(dt_done, 1)
                        pool.wait_ge(dt_done, at(s + 1))
                        pool.wait_ge(du_st, at(16 * s))
                        nc.gpsimd.tensor_tensor(duo[:, :], dto[:, :], U[:, m, :], ALU.mult).then_inc(du_done, 1)
                    if ffn and n == 54:
                        pool.wait_ge(n2, at(a + 1))
                        nc.gpsimd.tensor_tensor(X1[:, :, :], X1[:, :, :], XA[:, :, :], ALU.add).then_inc(r_done, 1)

            steps(pool, step)

        @block.tensor
        def _(pe):
            def project(q, m, col, done):
                for k in range(KM):
                    last = nc.tensor.matmul(pP[m % 2][:, :], c["Win"][:, k, col + m * P:col + (m + 1) * P], hT[:, k, :],
                                            start=(k == 0), stop=(k == KM - 1))
                last.then_inc(done, 1)

            def project_u(weight, m, bank, done):
                for k in range(KI):
                    last = nc.tensor.matmul(pP[bank][:, :], weight[:, k, m * P:(m + 1) * P], U[:, k, :],
                                            start=(k == 0), stop=(k == KI - 1))
                last.then_inc(done, 1)

            def transpose(i, done):
                for j in range(PAIR):
                    for k in range(KM):
                        last = nc.tensor.transpose(pA[i][:, k, j * P:(j + 1) * P], XN[:, i * PAIR + j, k * P:(k + 1) * P], c["ident"][:, :])
                last.then_inc(done, 1)

            def feed_forward(i, done):
                for j in range(PAIR):
                    lo = (i * PAIR + j) * P
                    nc.tensor.matmul(pA[i][:, j, :], c["ones"][:, :], c["bias"][:, :], start=True, stop=False)
                    for k in range(KM):
                        last = nc.tensor.matmul(pA[i][:, j, :], XNT[:, k, lo:lo + P], c["Wf"][:, k, :], start=False, stop=(k == KM - 1))
                last.then_inc(done, 1)

            def step(b, scan, close, proj, ffn):
                c_, q, a = b - 1, b + 1, b + 2
                for n in range(GN):
                    blk, k = n // KI, n % KI
                    if scan and blk == 0:
                        pe.wait_ge(u_done, at(KI * b + k + 1))
                        pe.wait_ge(gated, at(KI * b - KI + k + 1))
                        nc.tensor.matmul(Y[k][:, :], c["diagD"][:, k, :], U[:, k, :], start=True, stop=False).then_inc(skip, 1)
                    if scan:
                        pe.wait_ge(times_c, at(GN * b + n + 1))
                        for j in range(GS):
                            last = nc.tensor.matmul(Y[k][:, :], c["ident"][:, :], H[:, n % HR, j, :],
                                                    start=False, stop=(blk == NBLK - 1 and j == GS - 1))
                        last.then_inc(summed, 1)
                    if proj and n in (0, 1):
                        pe.wait_ge(h_out, at(2 * q + 2))
                        pe.wait_ge(relu_done, at(KI * q))
                        project(q, n, 0, mm_x)
                    if close and n in (5, 6):
                        i = n - 5
                        pe.wait_ge(gated, at(KI * c_ + KI))
                        pe.wait_ge(h_out, at(2 * ffns(b)))
                        for j in range(PAIR):
                            for k_ in range(KI):
                                last = nc.tensor.matmul(pA[i][:, j, :], YG[:, k_, (i * PAIR + j) * P:(i * PAIR + j + 1) * P],
                                                        c["Wout"][:, k_, :], start=(k_ == 0), stop=(k_ == KI - 1))
                        last.then_inc(y_mm, 1)
                    if proj and n in (7, 8):
                        pe.wait_ge(xs_out, at(KI * q + n - 6))
                        project(q, n - 5, 0, mm_x)
                    if proj and n in (13, 14):
                        pe.wait_ge(xs_out, at(KI * q + n - 10))
                        project(q, n - 13, DI, mm_z)
                    if close and n in (18, 19):
                        pe.wait_ge(nc_done, at(c_ + 1))
                        pe.wait_ge(x2_done, at(2 * c_ + 2))
                        transpose(n - 18, tc)
                    if proj and n in (20, 21):
                        pe.wait_ge(z_done, at(KI * q + n - 19))
                        project(q, n - 18, DI, mm_z)
                    if close and n in (24, 25):
                        pe.wait_ge(tc_out, at(2 * c_ + n - 23))
                        feed_forward(n - 24, ffnc)
                    if proj and n == 26:
                        pe.wait_ge(u_done, at(KI * q + KI))
                        pe.wait_ge(z_done, at(KI * q + 3))
                        project_u(c["bc_w"], 0, 0, mm_bc)
                    if proj and n in (28, 33, 35, 41):
                        if n == 28:
                            pe.wait_ge(z_done, at(KI * q + 4))
                        elif n == 33:
                            pe.wait_ge(bc_out, at(q + 1))
                        else:
                            pe.wait_ge(relu_done, at(KI * q + (1 if n == 35 else 2)))
                        m = (28, 33, 35, 41).index(n)
                        project_u(c["dt_w"], m, (m + 1) % 2, mm_dt)
                    if ffn and n in (35, 36):
                        pe.wait_ge(n1, at(a + 1))
                        pe.wait_ge(h_out, at(2 * a))
                        pe.wait_ge(o_done, at(2 * a - 4))
                        transpose(n - 35, t1)
                    if ffn and n in (42, 43):
                        pe.wait_ge(t1_out, at(2 * a + n - 41))
                        feed_forward(n - 42, ffn1)
                    if ffn and n in (58, 59):
                        pe.wait_ge(n3, at(a + 1))
                        pe.wait_ge(x1_done, at(2 * a + 2))
                        transpose(n - 58, t2)

            steps(pe, step)


def macaron(nc, w, out):
    dram = {"x": w["x"], "out": out}
    for name, shape in (("r", [NB, T, DM]), ("z", [NB, DI, T]), ("dt", [NB, DI, T]), ("du", [NB, DI, T]), ("bc", [NB, 2 * DS, T])):
        dram[name] = nc.dram_tensor("scratch_" + name, shape, fp32).ap()
    with ExitStack() as ctx:
        sb, _, _ = tools(nc, ctx)
        c = {n: sb("w_" + n, s) for n, s in (
            ("ident", [P, P]), ("diagD", [P, KI, P]), ("negA", [P, KI, DS]), ("Wf", [P, KM, DM]), ("bias", [1, DM]), ("ones", [1, P]),
            ("conv_w", [P, KI, DC]), ("conv_b", [P, KI]), ("dt_b", [P, KI]), ("D", [P, KI]), ("norm_w", [P, KM]), ("norm_b", [P, KM]),
            ("Wout", [P, KI, DM]), ("Win", [P, KM, 2 * DI]), ("dt_w", [P, KI, DI]), ("bc_w", [P, KI, 2 * DS]))}
        with ExitStack() as own:
            constants(nc, *tools(nc, own), w, c)
        with ExitStack() as own:
            counters = []
            sb, pb, sem = tools(nc, own, counters)
            layers(nc, sb, pb, sem, counters, c, dram)


def kernel(**inputs):
    import numpy as np
    import concourse.bacc as bacc
    from concourse.bass_utils import run_bass_kernel_spmd

    given = {n.split("_", 2)[2] if not n.endswith("kernel") else "kernel": np.asarray(a) for n, a in inputs.items()}
    given["aT"] = given.pop("a").T
    nc = bacc.Bacc("TRN2", target_bir_lowering=False, num_devices=1)
    arrays, w = {}, {}
    for n, a in given.items():
        arrays["in_" + n] = np.ascontiguousarray(a)
        w[n] = nc.dram_tensor("in_" + n, a.shape, mybir.dt.from_np(a.dtype), kind="ExternalInput").ap()
    out = nc.dram_tensor("out", (NB, T, DM), fp32, kind="ExternalOutput").ap()
    macaron(nc, w, out)
    r = run_bass_kernel_spmd(nc, [arrays], core_ids=[0])
    return r.results[0]["out"]
```

```python
from contextlib import ExitStack

import concourse.bass as bass
from concourse import mybir

P = 128
NB, T, DM = 16, 512, 256
DI, DS, DC = 512, 64, 4
RANK = 16
EPS = 1e-5
QMAX = 7.0
ROUND = 12582912.0
KM, KI, NJ = DM // P, DI // P, T // P
GS = 4
NBLK = DS // GS
GN = NBLK * KI
START = 48
DAR, HR = 2, 4
PAIR = NJ // 2

fp32 = mybir.dt.float32
ALU = mybir.AluOpType
ACT = mybir.ActivationFunctionType
AX = mybir.AxisListType


SPS = {"load r": (2,), "load x": (5,), "store B, C": (23,), "store dt": (27, 33, 39, 45), "store z": (28, 34, 40, 47),
       "load z0, z1": (28, 29), "store out": (31,), "store r": (52,)}
ACTS = {"xs": (4, 6, 12, 14), "u": (8, 10, 16, 18), "B, C": (20,), "dt": (23, 29, 35, 41), "z": (26, 32, 38, 44),
        "norm c": (14, 15, 17), "norm 1": (9, 11, 13), "norm 2": (45, 46, 47), "norm 3": (52, 53, 54),
        "turn c": (21, 24), "turn 1": (33, 36), "turn 3": (59, 62)}
DVES = {"x2": (8, 11), "norm c": (18,), "out": (26, 29), "norm 1": (23,), "x1": (38, 41), "norm 2": (48,), "norm 3": (55,),
        "soft": (24, 30, 36, 42)}
POOLS = {"dt": (25, 31, 37, 43), "r": (50,)}
PES = {"xs": (0, 2, 8, 10), "conv": (4, 6, 12, 14), "B, C": (16,), "dt": (19, 25, 31, 37), "z": (22, 28, 34, 40),
       "y": (5, 8), "turn c": (17, 20), "ffn c": (23, 26), "turn 1": (29, 32), "ffn 1": (35, 38), "turn 3": (55, 58)}
SPS0 = SPS | {"store z": (60, 61, 62, 63), "load x": (0,), "store r": (24,)}
ACTS0 = ACTS | {"z": (42, 43, 44, 45), "norm 1": (5, 5, 5), "turn 1": (9, 11), "norm 2": (17, 17, 17), "norm 3": (21, 21, 21), "turn 3": (46, 47)}
DVES0 = DVES | {"norm 1": (5,), "x1": (12, 13), "norm 2": (19,), "norm 3": (22,)}
POOLS0 = POOLS | {"r": (20,)}
PES0 = PES | {"z": (38, 39, 40, 41), "turn 1": (5, 7), "ffn 1": (9, 11), "turn 3": (42, 43)}


def at(n):
    return START + n


def begin(nc, counters):
    with nc.Block() as block:
        @block.sync
        def _(sp):
            for s in counters:
                sp.sem_inc(s, START)


def tools(nc, ctx, counters=None):
    def sb(name, shape, dt=fp32):
        return ctx.enter_context(nc.sbuf_tensor(name, shape, dt))

    def pb(name, shape, dt=fp32):
        return ctx.enter_context(nc.psum_tensor(name, shape, dt))

    def sem(name):
        s = ctx.enter_context(nc.semaphore(name))
        if counters is not None:
            counters.append(s)
        return s

    return sb, pb, sem


def constants(nc, sb, pb, sem, w, c):
    wk, aT, lb = sb("wk", [P, KM, DM]), sb("aT", [RANK, DM]), sb("lb", [RANK, DM])
    wabs, wq = sb("wabs", [P, KM, DM]), sb("wq", [P, KM, DM])
    mx, mx1, one, sc, alog = sb("mx", [P, 1]), sb("mx1", [1, 1]), sb("one", [1, P]), sb("sc", [P, 4]), sb("alog", [P, KI, DS])
    biasr = sb("biasr", [1, DM])
    pm, pab = pb("pm", [P, 512]), pb("pab", [P, KM, DM])
    k_small, k_big, k_id, k_abs, k_chain = sem("k_small"), sem("k_big"), sem("k_id"), sem("k_abs"), sem("k_chain")
    k_row, k_col, k_ab, k_one, k_expA, k_d = sem("k_row"), sem("k_col"), sem("k_ab"), sem("k_one"), sem("k_expA"), sem("k_d")

    with nc.Block() as block:
        @block.sync
        def _(sp):
            small = [(wk[:, :, :], w["kernel"].rearrange("(k p) f -> p k f", p=P)), (aT[:, :], w["aT"]), (lb[:, :], w["b"]),
                     (biasr[:, :], w["bias"].rearrange("(o f) -> o f", o=1)),
                     (alog[:, :, :], w["A_log"].rearrange("(k p) s -> p k s", p=P)),
                     (c["conv_w"][:, :, :], w["conv_w"].rearrange("(k p) o j -> p k (o j)", p=P))]
            small += [(c[n][:, :], w[n].rearrange("(k p) -> p k", p=P)) for n in ("conv_b", "dt_b", "D", "norm_w", "norm_b")]
            with nc.allow_non_contiguous_dma(reason="a few KiB, once"):
                for dst, src in small:
                    sp.dma_start(dst, src).then_inc(k_small, 16)
            for dst, src in ((c["Win"][:, :, :], w["Win"].rearrange("(k p) m -> p k m", p=P)),
                             (c["dt_w"][:, :, :], w["dt_w"].rearrange("(k p) m -> p k m", p=P)),
                             (c["bc_w"][:, :, 0:DS], w["Bp"].rearrange("(k p) m -> p k m", p=P)),
                             (c["bc_w"][:, :, DS:2 * DS], w["Cp"].rearrange("(k p) m -> p k m", p=P)),
                             (c["Wout"][:, :, :], w["Wout"].rearrange("(k p) m -> p k m", p=P))):
                sp.dma_start(dst, src).then_inc(k_big, 16)
            sp.wait_ge(k_big, 5 * 16)
            sp.wait_ge(k_small, 11 * 16)

        @block.gpsimd
        def _(pool):
            nc.gpsimd.memset(c["ident"][:, :], 0.0).then_inc(k_id, 1)
            pool.wait_ge(k_id, 1)
            nc.gpsimd.affine_select(out=c["ident"][:, :], in_=c["ident"][:, :], compare_op=ALU.not_equal, fill=1.0,
                                    base=0, pattern=[[-1, P]], channel_multiplier=1).then_inc(k_id, 1)

        @block.scalar
        def _(act):
            act.wait_ge(k_small, 11 * 16)
            nc.scalar.activation(wabs[:, :, :], wk[:, :, :], ACT.Abs).then_inc(k_abs, 1)
            nc.scalar.activation(c["negA"][:, :, :], alog[:, :, :], ACT.Exp).then_inc(k_expA, 1)

        @block.tensor
        def _(pe):
            pe.wait_ge(k_id, 2)
            pe.wait_ge(k_chain, 1)
            nc.tensor.matmul(pm[0:1, 0:P], mx[:, :], c["ident"][:, :], start=True, stop=True).then_inc(k_row, 1)
            pe.wait_ge(k_one, 1)
            pe.wait_ge(k_chain, 2)
            nc.tensor.matmul(pm[:, P:P + 1], one[:, :], mx1[:, :], start=True, stop=True).then_inc(k_col, 1)
            pe.wait_ge(k_small, 11 * 16)
            for k in range(KM):
                nc.tensor.matmul(pab[:, k, :], aT[:, k * P:(k + 1) * P], lb[:, :], start=(k == 0), stop=(k == KM - 1),
                                 skip_group_check=True).then_inc(k_ab, 1)

        @block.vector
        def _(dve):
            n = [0]

            def link(ins):
                n[0] += 1
                ins.then_inc(k_chain, 1)
                dve.wait_ge(k_chain, n[0])

            nc.vector.memset(one[:, :], 1.0).then_inc(k_one, 1)
            dve.wait_ge(k_abs, 1)
            link(nc.vector.reduce_max(mx[:, :], wabs[:, :, :].rearrange("p k f -> p (k f)"), AX.X))
            dve.wait_ge(k_row, 1)
            link(nc.vector.reduce_max(mx1[:, :], pm[0:1, 0:P], AX.X))
            dve.wait_ge(k_col, 1)
            link(nc.vector.tensor_scalar(sc[:, 0:1], pm[:, P:P + 1], 1.0 / QMAX, None, ALU.mult))
            link(nc.vector.reciprocal(sc[:, 1:2], sc[:, 0:1]))
            link(nc.vector.tensor_scalar(sc[:, 2:3], sc[:, 0:1], 0.5, None, ALU.mult))
            link(nc.vector.tensor_scalar(wq[:, :, :], wk[:, :, :], sc[:, 1:2], ROUND, ALU.mult, ALU.add))
            link(nc.vector.tensor_scalar(wabs[:, :, :], wq[:, :, :], ROUND, QMAX, ALU.subtract, ALU.min))
            link(nc.vector.tensor_scalar(wq[:, :, :], wabs[:, :, :], -8.0, sc[:, 2:3], ALU.max, ALU.mult))
            dve.wait_ge(k_ab, KM)
            link(nc.vector.scalar_tensor_tensor(out=c["Wf"][:, :, :], in0=pab[:, :, :], scalar=0.5, in1=wq[:, :, :],
                                                op0=ALU.mult, op1=ALU.add))
            dve.wait_ge(k_small, 11 * 16)
            link(nc.vector.tensor_scalar(c["bias"][:, :], biasr[:, :], 0.5, None, ALU.mult))
            link(nc.vector.tensor_copy(c["ones"][:, :], one[:, :]))
            dve.wait_ge(k_expA, 1)
            link(nc.vector.tensor_scalar(c["negA"][:, :, :], c["negA"][:, :, :], -1.0, None, ALU.mult))
            dve.wait_ge(k_id, 2)
            for k in range(KI):
                for j in range(DC):
                    nc.vector.tensor_scalar(c["taps"][:, k, j, :], c["ident"][:, :], c["conv_w"][:, k, j:j + 1], None, ALU.mult).then_inc(k_d, 1)
            for k in range(KI):
                nc.vector.tensor_scalar(c["diagD"][:, k, :], c["ident"][:, :], c["D"][:, k:k + 1], None, ALU.mult).then_inc(k_d, 1)


def mean_of(nc, act, tag, root, x, junk, mean, seq):
    act.wait_ge(root, at(seq))
    for j in range(NJ):
        last = nc.scalar.activation(junk[:, j, :], x[:, j, :], ACT.Copy, scale=-1.0 / DM, accum_out=mean[:, j:j + 1])
    last.then_inc(tag, 1)


def squares_of(nc, act, tag, x, junk, mean, var, seq):
    act.wait_ge(tag, at(2 * seq + 1))
    for j in range(NJ):
        last = nc.scalar.activation(junk[:, j, :], x[:, j, :], ACT.Square, bias=mean[:, j:j + 1], accum_out=var[:, j:j + 1])
    last.then_inc(tag, 1)


def root_of(nc, act, tag, root, var, sd, seq):
    act.wait_ge(tag, at(2 * seq + 2))
    nc.scalar.activation(sd[:, :], var[:, :], ACT.Sqrt, scale=1.0 / DM, bias=EPS).then_inc(root, 1)


def normalize(nc, dve, root, flip, x, out, mean, sd, rs, done, seq):
    dve.wait_ge(root, at(seq + 1))
    nc.vector.reciprocal(rs[:, :], sd[:, :]).then_inc(flip, 1)
    dve.wait_ge(flip, at(seq + 1))
    for j in range(NJ):
        last = nc.vector.tensor_scalar(out[:, j, :], x[:, j, :], mean[:, j:j + 1], rs[:, j:j + 1], ALU.add, ALU.mult)
    last.then_inc(done, 1)


def layers(nc, sb, pb, sem, counters, c, dram):
    X, X1, XA = sb("X", [P, NJ, DM]), sb("X1", [P, NJ, DM]), sb("XA", [P, NJ, DM])
    X2 = sb("X2", [P, NJ, DM])
    XN, XNT = sb("XN", [P, NJ, DM]), sb("XNT", [P, KM, T])
    junk = sb("junk", [P, NJ, DM], mybir.dt.bfloat16)
    norm1, norm2, norm3, normc = ([sb(f"{what}{i}", [P, NJ]) for what in ("mean", "var", "sd", "rs")] for i in ("1", "2", "3", "c"))
    hT, U = sb("hT", [P, KM, T]), sb("U", [P, KI, T])
    xs = sb("xs", [P, 2, DC - 1 + T])
    zo, BC = sb("zo", [P, 2, T]), sb("BC", [P, T])
    absv, ev, lnv, ev1, relu = (sb(n, [P, T]) for n in ("absv", "ev", "lnv", "ev1", "relu"))
    dto, duo = sb("dto", [P, T]), sb("duo", [P, T])
    DT, DU, ZL = sb("DT", [P, KI, T]), sb("DU", [P, KI, T]), sb("ZL", [P, 2, T])
    Bb, Cb = sb("Bb", [P, 2, GS, T]), sb("Cb", [P, 2, GS, T])
    dA, H = sb("dA", [P, DAR, GS, T]), sb("H", [P, HR, GS, T])
    YG = sb("YG", [P, KI, T])
    Y = [pb(f"Y{k}", [P, T]) for k in range(KI)]
    pUB = pb("pUB", [P, 2, T])
    pP = pb("pP", [P, T])
    pA = pb("pA", [P, 2, DM])

    x_in, x1_done, r_done, r_st, h_out = sem("x_in"), sem("x1_done"), sem("r_done"), sem("r_st"), sem("h_out")
    (ln1, root1, flip1, n1), (ln2, root2, flip2, n2), (ln3, root3, flip3, n3), (lnc, rootc, flipc, nc_done) = (
        [sem(f"{what}{i}") for what in ("ln", "root", "flip", "n")] for i in ("1", "2", "3", "c"))
    t1, t1_out, ffn1, t2 = sem("t1"), sem("t1_out"), sem("ffn1"), sem("t2")
    r_in, y_mm, x2_done = sem("r_in"), sem("y_mm"), sem("x2_done")
    tc, tc_out, ffnc, o_done, o_st = sem("tc"), sem("tc_out"), sem("ffnc"), sem("o_done"), sem("o_st")
    zero, mm_x, mm_z, mm_bc, mm_dt = sem("zero"), sem("mm_x"), sem("mm_z"), sem("mm_bc"), sem("mm_dt")
    xs_out, conv, u_done, z_done, bc_out = sem("xs_out"), sem("conv"), sem("u_done"), sem("z_done"), sem("bc_out")
    abs_done, relu_done, exp_done, ln_done, one_done = sem("abs_done"), sem("relu_done"), sem("exp_done"), sem("ln_done"), sem("one_done")
    soft1, soft2, dt_done, du_done = sem("soft1"), sem("soft2"), sem("dt_done"), sem("du_done")
    z_st, bc_st, dt_st, du_st = [sem(f"z_st{i}") for i in range(2)], sem("bc_st"), sem("dt_st"), sem("du_st")
    z_in, du_in = [sem(f"z_in{i}") for i in range(2)], [sem(f"du_in{k}") for k in range(KI)]
    bc_in = [sem(f"bc_in{i}") for i in range(2)]
    decay, forced, state_done, times_c, summed, skip, gated = (sem(n) for n in ("decay", "forced", "state_done", "times_c", "summed", "skip", "gated"))

    def tile_of(d, b, k):
        return dram[d][bass.ds(b, 1), k * P:(k + 1) * P, :].rearrange("o p t -> p (o t)")

    def tokens_of(d, b):
        return dram[d][bass.ds(b, 1)].rearrange("o (j p) d -> p (o j) d", p=P)

    def ffns(b):
        return min(b + 2, NB) if isinstance(b, int) else b + 2

    def steps(engine, step):
        step(-2, False, False, False, True)
        step(-1, False, False, True, True)
        step(0, True, False, True, True)
        with engine.Fori(1, NB - 2) as b:
            step(b, True, True, True, True)
        step(NB - 2, True, True, True, False)
        step(NB - 1, True, True, False, False)
        step(NB, False, True, False, False)

    begin(nc, counters)
    with nc.Block() as block:
        @block.sync
        def _(sp):
            def load_block(b, blk, groups):
                for dst, lo, used, each in ((Bb, 0, state_done, GS), (Cb, DS, times_c, 2)):
                    sp.wait_ge(used, at(each * groups))
                    src = dram["bc"][bass.ds(b, 1), lo + GS * blk:lo + GS * (blk + 1), :].rearrange("o s t -> o (s t)")
                    sp.dma_start(dst[:, blk % 2].rearrange("p s t -> p (s t)"), src.to_broadcast([P, GS * T])).then_inc(bc_in[blk % 2], 16)

            def load_z(b, k):
                sp.wait_ge(gated, at(KI * b + k - 1))
                sp.wait_ge(z_st[k % 2], at(16 * (2 * b + k // 2 + 1)))
                sp.dma_start(ZL[:, k % 2, :], tile_of("z", b, k)).then_inc(z_in[k % 2], 16)

            def load_du(b, k):
                sp.wait_ge(decay, at(GN * b - KI + k + 1))
                sp.wait_ge(dt_st, at(16 * (KI * b + k + 1)))
                sp.dma_start(DT[:, k, :], tile_of("dt", b, k)).then_inc(du_in[k], 16)
                sp.wait_ge(state_done, at(GS * (GN * b - KI + k + 1)))
                sp.wait_ge(du_st, at(16 * (KI * b + k + 1)))
                sp.dma_start(DU[:, k, :], tile_of("du", b, k)).then_inc(du_in[k], 16)

            def store_z(q, m):
                sp.wait_ge(z_done, at(KI * q + m + 1))
                sp.dma_start(tile_of("z", q, m), zo[:, m % 2, :]).then_inc(z_st[m % 2], 16)

            def store_du(q, m):
                sp.wait_ge(dt_done, at(KI * q + m + 1))
                sp.dma_start(tile_of("dt", q, m), dto[:, :]).then_inc(dt_st, 16)
                sp.wait_ge(du_done, at(KI * q + m + 1))
                sp.dma_start(tile_of("du", q, m), duo[:, :]).then_inc(du_st, 16)

            def step(b, scan, close, proj, ffn):
                c_, q, a = b - 1, b + 1, b + 2
                when = SPS if scan or close else SPS0
                for n in range(GN):
                    blk, k = n // KI, n % KI
                    if close and n == 0:
                        sp.wait_ge(o_st, at(16 * c_))
                        load_z(c_, 2)
                        load_z(c_, 3)
                    if scan and k == 0 and blk < NBLK - 1:
                        load_block(b, blk + 1, GN * b + n)
                    if close and n in when["load r"]:
                        sp.wait_ge(r_st, at(16 * c_ + 16))
                        sp.dma_start(X2[:, :, :], tokens_of("r", c_)).then_inc(r_in, 16)
                    if proj and n in when["store z"]:
                        store_z(q, when["store z"].index(n))
                    if ffn and n in when["load x"]:
                        sp.wait_ge(x1_done, at(2 * a))
                        sp.dma_start(X[:, :, :], tokens_of("x", a)).then_inc(x_in, 16)
                    if scan and n in when["load z0, z1"]:
                        load_z(b, when["load z0, z1"].index(n))
                    if close and n in when["store out"]:
                        sp.wait_ge(o_done, at(2 * c_ + 2))
                        sp.dma_start(tokens_of("out", c_), X2[:, :, :]).then_inc(o_st, 16)
                    if proj and n in when["store B, C"]:
                        sp.wait_ge(bc_out, at(q + 1))
                        sp.dma_start(dram["bc"][bass.ds(q, 1)].rearrange("o p t -> p (o t)"), BC[:, :]).then_inc(bc_st, 16)
                    if proj and n in when["store dt"]:
                        store_du(q, when["store dt"].index(n))
                    if ffn and n in when["store r"]:
                        sp.wait_ge(r_done, at(a + 1))
                        sp.dma_start(tokens_of("r", a), X1[:, :, :]).then_inc(r_st, 16)
                    if proj and n == GN - KI:
                        sp.wait_ge(bc_st, at(16 * q + 16))
                        load_block(q, 0, GN * q - KI)
                    if proj and n >= GN - KI:
                        load_du(q, k)

            steps(sp, step)
            sp.wait_ge(o_st, at(16 * NB))

        @block.scalar
        def _(act):
            def take_xs(q, m):
                act.wait_ge(mm_x, at(KI * q + m + 1))
                act.wait_ge(conv, at(KI * q + m - 1))
                nc.scalar.activation(xs[:, m % 2, DC - 1:], pP[:, :], ACT.Copy).then_inc(xs_out, 1)

            def silu_u(q, m):
                act.wait_ge(conv, at(KI * q + m + 1))
                act.wait_ge(mm_dt, at(KI * q))
                act.wait_ge(du_done, at(KI * q))
                act.wait_ge(skip, at(KI * q))
                nc.scalar.activation(U[:, m, :], pP[:, :], ACT.Silu, bias=c["conv_b"][:, m:m + 1]).then_inc(u_done, 1)

            def silu_z(q, m):
                act.wait_ge(mm_z, at(KI * q + m + 1))
                act.wait_ge(z_st[m % 2], at(16 * (2 * q + m // 2)))
                nc.scalar.activation(zo[:, m % 2, :], pP[:, :], ACT.Silu).then_inc(z_done, 1)

            def softplus(q, m):
                n = KI * q + m
                v = pP[:, :]
                act.wait_ge(mm_dt, at(n + 1))
                act.wait_ge(dt_done, at(n))
                act.wait_ge(exp_done, at(n))
                nc.scalar.activation(absv[:, :], v, ACT.Abs, bias=c["dt_b"][:, m:m + 1]).then_inc(abs_done, 1)
                nc.scalar.activation(relu[:, :], v, ACT.Relu, bias=c["dt_b"][:, m:m + 1]).then_inc(relu_done, 1)
                act.wait_ge(abs_done, at(n + 1))
                nc.scalar.activation(ev[:, :], absv[:, :], ACT.Exp, scale=-1.0).then_inc(exp_done, 1)
                act.wait_ge(exp_done, at(n + 1))
                nc.scalar.activation(lnv[:, :], ev[:, :], ACT.Ln, bias=1.0).then_inc(ln_done, 1)
                nc.scalar.activation(ev1[:, :], ev[:, :], ACT.Copy, bias=1.0).then_inc(one_done, 1)

            def step(b, scan, close, proj, ffn):
                c_, q, a = b - 1, b + 1, b + 2
                when = ACTS if scan or close else ACTS0
                for n in range(GN):
                    blk, k = n // KI, n % KI
                    if scan:
                        if blk == 0:
                            act.wait_ge(du_in[k], at(32 * b + 32))
                        act.wait_ge(state_done, at(GS * (GN * b + n + 1 - DAR)))
                        for j in range(GS):
                            last = nc.scalar.activation(dA[:, n % DAR, j, :], DT[:, k, :], ACT.Exp,
                                                        scale=c["negA"][:, k, GS * blk + j:GS * blk + j + 1])
                        last.then_inc(decay, 1)
                    if proj and n in when["xs"]:
                        take_xs(q, when["xs"].index(n))
                    if proj and n in when["u"]:
                        silu_u(q, when["u"].index(n))
                    if close and n == when["norm c"][0]:
                        act.wait_ge(x2_done, at(2 * c_ + 2))
                        act.wait_ge(nc_done, at(c_))
                        mean_of(nc, act, lnc, rootc, X2, junk, normc[0], c_)
                    if close and n == when["norm c"][1]:
                        squares_of(nc, act, lnc, X2, junk, normc[0], normc[1], c_)
                    if close and n == when["norm c"][2]:
                        root_of(nc, act, lnc, rootc, normc[1], normc[2], c_)
                    if close and n in when["turn c"]:
                        i = when["turn c"].index(n)
                        act.wait_ge(tc, at(2 * c_ + i + 1))
                        nc.scalar.activation(XNT[:, :, i * PAIR * P:(i + 1) * PAIR * P], pA[:, :, :], ACT.Copy).then_inc(tc_out, 1)
                    if proj and n in when["z"]:
                        silu_z(q, when["z"].index(n))
                    if ffn and n == when["norm 1"][0]:
                        act.wait_ge(x_in, at(16 * a + 16))
                        act.wait_ge(n1, at(a))
                        mean_of(nc, act, ln1, root1, X, junk, norm1[0], a)
                    if ffn and n == when["norm 1"][1]:
                        squares_of(nc, act, ln1, X, junk, norm1[0], norm1[1], a)
                    if ffn and n == when["norm 1"][2]:
                        root_of(nc, act, ln1, root1, norm1[1], norm1[2], a)
                    if proj and n in when["B, C"]:
                        act.wait_ge(mm_bc, at(q + 1))
                        act.wait_ge(bc_st, at(16 * q))
                        nc.scalar.activation(BC[:, :], pP[:, :], ACT.Copy).then_inc(bc_out, 1)
                    if proj and n in when["dt"]:
                        softplus(q, when["dt"].index(n))
                    if ffn and n in when["turn 1"]:
                        i = when["turn 1"].index(n)
                        act.wait_ge(t1, at(2 * a + i + 1))
                        nc.scalar.activation(XNT[:, :, i * PAIR * P:(i + 1) * PAIR * P], pA[:, :, :], ACT.Copy).then_inc(t1_out, 1)
                    if ffn and n == when["norm 2"][0]:
                        act.wait_ge(x1_done, at(2 * a + 2))
                        act.wait_ge(n2, at(a))
                        mean_of(nc, act, ln2, root2, X1, junk, norm2[0], a)
                    if ffn and n == when["norm 2"][1]:
                        squares_of(nc, act, ln2, X1, junk, norm2[0], norm2[1], a)
                    if ffn and n == when["norm 2"][2]:
                        root_of(nc, act, ln2, root2, norm2[1], norm2[2], a)
                    if ffn and n == when["norm 3"][0]:
                        act.wait_ge(n2, at(a + 1))
                        act.wait_ge(n3, at(a))
                        mean_of(nc, act, ln3, root3, XA, junk, norm3[0], a)
                    if ffn and n == when["norm 3"][1]:
                        squares_of(nc, act, ln3, XA, junk, norm3[0], norm3[1], a)
                    if ffn and n == when["norm 3"][2]:
                        root_of(nc, act, ln3, root3, norm3[1], norm3[2], a)
                    if ffn and n in when["turn 3"]:
                        i = when["turn 3"].index(n)
                        act.wait_ge(t2, at(2 * a + i + 1))
                        for k_ in range(KM):
                            last = nc.scalar.activation(hT[:, k_, i * PAIR * P:(i + 1) * PAIR * P], pA[:, k_, :], ACT.Identity,
                                                        scale=c["norm_w"][:, k_:k_ + 1], bias=c["norm_b"][:, k_:k_ + 1])
                        last.then_inc(h_out, 1)

            act.wait_ge(zero, at(1))
            steps(act, step)

        @block.vector
        def _(dve):
            def step(b, scan, close, proj, ffn):
                c_, q, a = b - 1, b + 1, b + 2
                when = DVES if scan or close else DVES0
                for n in range(GN):
                    blk, k = n // KI, n % KI
                    if close and blk == 0:
                        dve.wait_ge(summed, at(GN * c_ + GN - KI + k + 1))
                        dve.wait_ge(z_in[k % 2], at(16 * (2 * c_ + k // 2 + 1)))
                        dve.wait_ge(y_mm, at(2 * c_))
                        nc.vector.tensor_tensor(YG[:, k, :], Y[k][:, :], ZL[:, k % 2, :], ALU.mult).then_inc(gated, 1)
                    if scan:
                        h = H[:, n % HR]
                        if blk == 0:
                            dve.wait_ge(du_in[k], at(32 * b + 32))
                        if k == 0:
                            dve.wait_ge(bc_in[blk % 2], at(32 * (b * (NBLK // 2) + blk // 2 + 1)))
                        dve.wait_ge(summed, at(GN * b + n + 1 - HR))
                        s = GS * (GN * b + n)
                        for j in range(0, GS, 2):
                            for i in range(j, j + 2):
                                dve.wait_ge(state_done, at(s + i - 1))
                                nc.vector.tensor_tensor(pUB[:, i % 2, :], Bb[:, blk % 2, i, :], DU[:, k, :], ALU.mult).then_inc(forced, 1)
                            if j == 0:
                                dve.wait_ge(decay, at(GN * b + n + 1))
                            for i in range(j, j + 2):
                                dve.wait_ge(forced, at(s + i + 1))
                                nc.vector.tensor_tensor_scan(h[:, i, :], dA[:, n % DAR, i, :], pUB[:, i % 2, :], 0.0,
                                                             ALU.mult, ALU.add).then_inc(state_done, 1)
                    if close and n in when["x2"]:
                        i = when["x2"].index(n)
                        dve.wait_ge(r_in, at(16 * c_ + 16))
                        dve.wait_ge(y_mm, at(2 * c_ + i + 1))
                        nc.vector.tensor_tensor(X2[:, 2 * i:2 * i + 2, :], X2[:, 2 * i:2 * i + 2, :], pA[:, :, :], ALU.add).then_inc(x2_done, 1)
                    if close and n in when["norm c"]:
                        dve.wait_ge(t2, at(2 * ffns(b)))
                        mean, _, sd, rs = normc
                        normalize(nc, dve, rootc, flipc, X2, XN, mean, sd, rs, nc_done, c_)
                    if close and n in when["out"]:
                        i = when["out"].index(n)
                        dve.wait_ge(ffnc, at(2 * c_ + i + 1))
                        nc.vector.tensor_tensor(X2[:, 2 * i:2 * i + 2, :], X2[:, 2 * i:2 * i + 2, :], pA[:, :, :], ALU.add).then_inc(o_done, 1)
                    if proj and n in when["soft"]:
                        m = KI * q + when["soft"].index(n)
                        dve.wait_ge(one_done, at(m + 1))
                        nc.vector.scalar_tensor_tensor(out=ev1[:, :], in0=ev1[:, :], scalar=-1.0, in1=ev[:, :],
                                                       op0=ALU.add, op1=ALU.subtract).then_inc(soft1, 1)
                    if ffn and n in when["norm 1"]:
                        dve.wait_ge(tc, at(2 * a - 4))
                        dve.wait_ge(t2, at(2 * a))
                        mean, _, sd, rs = norm1
                        normalize(nc, dve, root1, flip1, X, XN, mean, sd, rs, n1, a)
                    if ffn and n in when["x1"]:
                        i = when["x1"].index(n)
                        dve.wait_ge(ffn1, at(2 * a + i + 1))
                        dve.wait_ge(r_st, at(16 * a))
                        nc.vector.tensor_tensor(X1[:, 2 * i:2 * i + 2, :], X[:, 2 * i:2 * i + 2, :], pA[:, :, :], ALU.add).then_inc(x1_done, 1)
                    if ffn and n in when["norm 2"]:
                        dve.wait_ge(r_done, at(a))
                        mean, _, sd, rs = norm2
                        normalize(nc, dve, root2, flip2, X1, XA, mean, sd, rs, n2, a)
                    if ffn and n in when["norm 3"]:
                        dve.wait_ge(t1, at(2 * a + 2))
                        mean, _, sd, rs = norm3
                        normalize(nc, dve, root3, flip3, XA, XN, mean, sd, rs, n3, a)

            nc.vector.memset(xs[:, :, 0:DC - 1], 0.0).then_inc(zero, 1)
            dve.wait_ge(zero, at(1))
            steps(dve, step)

        @block.gpsimd
        def _(pool):
            def step(b, scan, close, proj, ffn):
                q, a = b + 1, b + 2
                when = POOLS if scan or close else POOLS0
                for n in range(GN):
                    blk, h = n // KI, H[:, n % HR]
                    if scan:
                        for j in range(0, GS, 2):
                            pool.wait_ge(state_done, at(GS * (GN * b + n) + j + 2))
                            nc.gpsimd.tensor_tensor(h[:, j:j + 2, :], h[:, j:j + 2, :], Cb[:, blk % 2, j:j + 2, :], ALU.mult).then_inc(times_c, 1)
                    if proj and n in when["dt"]:
                        m = when["dt"].index(n)
                        s = KI * q + m
                        pool.wait_ge(soft1, at(s + 1))
                        pool.wait_ge(ln_done, at(s + 1))
                        nc.gpsimd.tensor_tensor(lnv[:, :], lnv[:, :], ev1[:, :], ALU.subtract).then_inc(soft2, 1)
                        pool.wait_ge(soft2, at(s + 1))
                        pool.wait_ge(relu_done, at(s + 1))
                        pool.wait_ge(dt_st, at(16 * s))
                        nc.gpsimd.tensor_tensor(dto[:, :], lnv[:, :], relu[:, :], ALU.add).then_inc(dt_done, 1)
                        pool.wait_ge(dt_done, at(s + 1))
                        pool.wait_ge(du_st, at(16 * s))
                        nc.gpsimd.tensor_tensor(duo[:, :], dto[:, :], U[:, m, :], ALU.mult).then_inc(du_done, 1)
                    if ffn and n in when["r"]:
                        pool.wait_ge(n2, at(a + 1))
                        nc.gpsimd.tensor_tensor(X1[:, :, :], X1[:, :, :], XA[:, :, :], ALU.add).then_inc(r_done, 1)

            steps(pool, step)

        @block.tensor
        def _(pe):
            def project(q, m, col, done):
                for k in range(KM):
                    last = nc.tensor.matmul(pP[:, :], c["Win"][:, k, col + m * P:col + (m + 1) * P], hT[:, k, :],
                                            start=(k == 0), stop=(k == KM - 1))
                last.then_inc(done, 1)

            def convolve(q, m):
                pe.wait_ge(xs_out, at(KI * q + m + 1))
                for j in range(DC):
                    last = nc.tensor.matmul(pP[:, :], c["taps"][:, m, j, :], xs[:, m % 2, j:j + T], start=(j == 0), stop=(j == DC - 1))
                last.then_inc(conv, 1)

            def project_u(weight, m, done):
                for k in range(KI):
                    last = nc.tensor.matmul(pP[:, :], weight[:, k, m * P:(m + 1) * P], U[:, k, :],
                                            start=(k == 0), stop=(k == KI - 1))
                last.then_inc(done, 1)

            def transpose(i, done):
                for j in range(PAIR):
                    for k in range(KM):
                        last = nc.tensor.transpose(pA[:, k, j * P:(j + 1) * P], XN[:, i * PAIR + j, k * P:(k + 1) * P], c["ident"][:, :])
                last.then_inc(done, 1)

            def feed_forward(i, done):
                for j in range(PAIR):
                    lo = (i * PAIR + j) * P
                    nc.tensor.matmul(pA[:, j, :], c["ones"][:, :], c["bias"][:, :], start=True, stop=False)
                    for k in range(KM):
                        last = nc.tensor.matmul(pA[:, j, :], XNT[:, k, lo:lo + P], c["Wf"][:, k, :], start=False, stop=(k == KM - 1))
                last.then_inc(done, 1)

            def step(b, scan, close, proj, ffn):
                c_, q, a = b - 1, b + 1, b + 2
                when = PES if scan or close else PES0
                for n in range(GN):
                    blk, k = n // KI, n % KI
                    if scan and blk == 0:
                        pe.wait_ge(u_done, at(KI * b + k + 1))
                        pe.wait_ge(gated, at(KI * b - KI + k + 1))
                        nc.tensor.matmul(Y[k][:, :], c["diagD"][:, k, :], U[:, k, :], start=True, stop=False).then_inc(skip, 1)
                    if scan:
                        for j in range(GS):
                            if j % 2 == 0:
                                pe.wait_ge(times_c, at(2 * (GN * b + n) + j // 2 + 1))
                            last = nc.tensor.matmul(Y[k][:, :], c["ident"][:, :], H[:, n % HR, j, :],
                                                    start=False, stop=(blk == NBLK - 1 and j == GS - 1))
                        last.then_inc(summed, 1)
                    if proj and n in when["xs"]:
                        m = when["xs"].index(n)
                        if m == 0:
                            pe.wait_ge(h_out, at(2 * q + 2))
                            pe.wait_ge(z_done, at(KI * q))
                        pe.wait_ge(xs_out, at(KI * q + m))
                        pe.wait_ge(u_done, at(KI * q + (m if m == 2 else 0)))
                        project(q, m, 0, mm_x)
                    if proj and n in when["conv"]:
                        m = when["conv"].index(n)
                        pe.wait_ge(xs_out, at(KI * q + (m // 2) * 2 + 2))
                        pe.wait_ge(u_done, at(KI * q + m))
                        convolve(q, m)
                    if proj and n in when["B, C"]:
                        pe.wait_ge(u_done, at(KI * q + KI))
                        project_u(c["bc_w"], 0, mm_bc)
                    if proj and n in when["dt"]:
                        m = when["dt"].index(n)
                        pe.wait_ge(bc_out, at(q + 1))
                        pe.wait_ge(relu_done, at(KI * q + m))
                        if scan:
                            pe.wait_ge(z_done, at(KI * q + m))
                        project_u(c["dt_w"], m, mm_dt)
                    if proj and n in when["z"]:
                        m = when["z"].index(n)
                        pe.wait_ge(relu_done, at(KI * q + (m + 1 if scan else KI)))
                        pe.wait_ge(z_done, at(KI * q + m))
                        project(q, m, DI, mm_z)
                    if close and n in when["y"]:
                        i = when["y"].index(n)
                        pe.wait_ge(gated, at(KI * c_ + KI))
                        pe.wait_ge(h_out, at(2 * ffns(b)))
                        pe.wait_ge(x2_done, at(2 * c_ + i))
                        for j in range(PAIR):
                            for k_ in range(KI):
                                last = nc.tensor.matmul(pA[:, j, :], YG[:, k_, (i * PAIR + j) * P:(i * PAIR + j + 1) * P],
                                                        c["Wout"][:, k_, :], start=(k_ == 0), stop=(k_ == KI - 1))
                        last.then_inc(y_mm, 1)
                    if close and n in when["turn c"]:
                        i = when["turn c"].index(n)
                        pe.wait_ge(nc_done, at(c_ + 1))
                        pe.wait_ge(x2_done, at(2 * c_ + 2))
                        pe.wait_ge(tc_out, at(2 * c_ + i))
                        transpose(i, tc)
                    if close and n in when["ffn c"]:
                        i = when["ffn c"].index(n)
                        pe.wait_ge(tc_out, at(2 * c_ + 2))
                        pe.wait_ge(o_done, at(2 * c_ + i))
                        feed_forward(i, ffnc)
                    if ffn and n in when["turn 1"]:
                        i = when["turn 1"].index(n)
                        pe.wait_ge(n1, at(a + 1))
                        pe.wait_ge(h_out, at(2 * a))
                        pe.wait_ge(o_done, at(2 * a - 4))
                        pe.wait_ge(t1_out, at(2 * a + i))
                        transpose(i, t1)
                    if ffn and n in when["ffn 1"]:
                        i = when["ffn 1"].index(n)
                        pe.wait_ge(t1_out, at(2 * a + 2))
                        pe.wait_ge(x1_done, at(2 * a + i))
                        feed_forward(i, ffn1)
                    if ffn and n in when["turn 3"]:
                        i = when["turn 3"].index(n)
                        pe.wait_ge(n3, at(a + 1))
                        pe.wait_ge(x1_done, at(2 * a + 2))
                        pe.wait_ge(h_out, at(2 * a + i))
                        transpose(i, t2)

            steps(pe, step)


def macaron(nc, w, out):
    dram = {"x": w["x"], "out": out}
    for name, shape in (("r", [NB, T, DM]), ("z", [NB, DI, T]), ("dt", [NB, DI, T]), ("du", [NB, DI, T]), ("bc", [NB, 2 * DS, T])):
        dram[name] = nc.dram_tensor("scratch_" + name, shape, fp32).ap()
    with ExitStack() as ctx:
        sb, _, _ = tools(nc, ctx)
        c = {n: sb("w_" + n, s) for n, s in (
            ("ident", [P, P]), ("taps", [P, KI, DC, P]), ("diagD", [P, KI, P]), ("negA", [P, KI, DS]), ("Wf", [P, KM, DM]), ("bias", [1, DM]), ("ones", [1, P]),
            ("conv_w", [P, KI, DC]), ("conv_b", [P, KI]), ("dt_b", [P, KI]), ("D", [P, KI]), ("norm_w", [P, KM]), ("norm_b", [P, KM]),
            ("Wout", [P, KI, DM]), ("Win", [P, KM, 2 * DI]), ("dt_w", [P, KI, DI]), ("bc_w", [P, KI, 2 * DS]))}
        with ExitStack() as own:
            constants(nc, *tools(nc, own), w, c)
        with ExitStack() as own:
            counters = []
            sb, pb, sem = tools(nc, own, counters)
            layers(nc, sb, pb, sem, counters, c, dram)


def kernel(**inputs):
    import numpy as np
    import concourse.bacc as bacc
    from concourse.bass_utils import run_bass_kernel_spmd

    given = {n.split("_", 2)[2] if not n.endswith("kernel") else "kernel": np.asarray(a) for n, a in inputs.items()}
    given["aT"] = given.pop("a").T
    nc = bacc.Bacc("TRN2", target_bir_lowering=False, num_devices=1)
    arrays, w = {}, {}
    for n, a in given.items():
        arrays["in_" + n] = np.ascontiguousarray(a)
        w[n] = nc.dram_tensor("in_" + n, a.shape, mybir.dt.from_np(a.dtype), kind="ExternalInput").ap()
    out = nc.dram_tensor("out", (NB, T, DM), fp32, kind="ExternalOutput").ap()
    macaron(nc, w, out)
    r = run_bass_kernel_spmd(nc, [arrays], core_ids=[0])
    return r.results[0]["out"]
```
